# Optimizing a Trainium2 kernel written in Bass

```python
import numpy as np
import jax
import jax.numpy as jnp

def _softmax(x, axis=-1):
    return jax.nn.softmax(x, axis=axis)

def _gelu(x):
    return jax.nn.gelu(x, approximate=True)

def _silu(x):
    return jax.nn.silu(x)

def _sigmoid(x):
    return jax.nn.sigmoid(x)

def _layernorm(x, axis=-1, eps=1e-05):
    m = jnp.mean(x, axis=axis, keepdims=True)
    v = jnp.var(x, axis=axis, keepdims=True)
    return (x - m) / jnp.sqrt(v + eps)

def _scatter_add(tgt, idx, src, axis=0):
    return tgt.at[idx].add(src)

def _segment_sum(src, seg, n):
    return jax.ops.segment_sum(src, seg, n)
kernel_name = 'mk_conv_attn_hybrid_d2_conv_nhwc256_r4_dcdd28'

def setup_inputs(seed: int=0):
    np.random.seed(seed)
    _w = jnp.asarray

    def _rec_inputs():
        import jax
        import jax.numpy as jnp
        _gk = jax.random.key(seed)
        x = -0.0002091 + 1 * jax.random.normal(jax.random.fold_in(_gk, 1), (32, 56, 56, 64), jnp.float32)
        return x
    x = _rec_inputs()

    def _L0_conv_setup():
        import jax, jax.numpy as jnp
        import numpy as np
        DIM = 64
        HEADS = 8
        HEAD_DIM = DIM // HEADS
        WS = 7
        SHIFT = 3
        H = 56
        W = 56
        B = 32
        WA = WS * WS
        NWH, NWW = (H // WS, W // WS)
        NW = NWH * NWW

        def _make_attn_mask():
            img = np.zeros((H, W), dtype=np.float32)
            cnt = 0
            for hs in (slice(0, -WS), slice(-WS, -SHIFT), slice(-SHIFT, None)):
                for ws_ in (slice(0, -WS), slice(-WS, -SHIFT), slice(-SHIFT, None)):
                    img[hs, ws_] = cnt
                    cnt += 1
            mw = img.reshape(NWH, WS, NWW, WS).transpose(0, 2, 1, 3).reshape(-1, WA)
            diff = mw[:, None, :] - mw[:, :, None]
            return np.where(diff != 0, -100.0, 0.0).astype(np.float32)

        def _make_rel_index():
            coords = np.stack(np.meshgrid(np.arange(WS), np.arange(WS), indexing='ij')).reshape(2, -1)
            rel = coords[:, :, None] - coords[:, None, :]
            rel = rel.transpose(1, 2, 0) + (WS - 1)
            rel[..., 0] *= 2 * WS - 1
            return rel.sum(-1).astype(np.int32)

        def _ln(x, w, b, eps=1e-05):
            m = jnp.mean(x, axis=-1, keepdims=True)
            v = jnp.mean((x - m) ** 2, axis=-1, keepdims=True)
            return (x - m) * jax.lax.rsqrt(v + eps) * w + b
        key = jax.random.key(seed)
        ks = jax.random.split(key, 12)
        s = 0.02
        inp = {'x': jax.random.normal(ks[0], (B, H, W, DIM), dtype=jnp.float32), 'ln1_w': jnp.ones((DIM,), jnp.float32), 'ln1_b': jnp.zeros((DIM,), jnp.float32), 'qkv_w': s * jax.random.normal(ks[1], (3 * DIM, DIM), jnp.float32), 'qkv_b': jnp.zeros((3 * DIM,), jnp.float32), 'rpb_table': s * jax.random.normal(ks[2], ((2 * WS - 1) ** 2, HEADS), jnp.float32), 'proj_w': s * jax.random.normal(ks[3], (DIM, DIM), jnp.float32), 'proj_b': jnp.zeros((DIM,), jnp.float32), 'ln2_w': jnp.ones((DIM,), jnp.float32), 'ln2_b': jnp.zeros((DIM,), jnp.float32), 'fc1_w': s * jax.random.normal(ks[4], (4 * DIM, DIM), jnp.float32), 'fc1_b': jnp.zeros((4 * DIM,), jnp.float32), 'ln3_w': jnp.ones((4 * DIM,), jnp.float32), 'ln3_b': jnp.zeros((4 * DIM,), jnp.float32), 'fc2_w': s * jax.random.normal(ks[5], (DIM, 4 * DIM), jnp.float32), 'fc2_b': jnp.zeros((DIM,), jnp.float32), 'attn_mask': jnp.asarray(_make_attn_mask()), 'rel_index': jnp.asarray(_make_rel_index())}
        return inp
    _L0_conv_all = _L0_conv_setup()
    _L0_conv_in = {k: v for k, v in _L0_conv_all.items() if k in ('ln1_w', 'ln1_b', 'qkv_w', 'qkv_b', 'rpb_table', 'proj_w', 'proj_b', 'ln2_w', 'ln2_b', 'fc1_w', 'fc1_b', 'ln3_w', 'ln3_b', 'fc2_w', 'fc2_b', 'attn_mask', 'rel_index')}
    del _L0_conv_all

    def _L1_attn_setup():
        import jax, jax.numpy as jnp
        import numpy as np
        MIDC = 64
        HEADS = 16
        HEADC = MIDC // HEADS
        EPS = 1e-05

        def _layernorm(x, w, b):
            mean = jnp.mean(x, axis=-1, keepdims=True)
            std = jnp.std(x, axis=-1, keepdims=True, ddof=1)
            return w * (x - mean) / (std + EPS) + b
        key = jax.random.key(seed)
        ks = jax.random.split(key, 3)
        B, HW = (8, 4096)
        x = jax.random.normal(ks[0], (B, HW, MIDC), dtype=jnp.float32)
        W_qkv = jax.random.normal(ks[1], (3 * MIDC, MIDC), dtype=jnp.float32) * 0.02
        b_qkv = jnp.zeros((3 * MIDC,), dtype=jnp.float32)
        kln_w = jnp.ones((HEADS, 1, HEADC), dtype=jnp.float32)
        kln_b = jnp.zeros((HEADS, 1, HEADC), dtype=jnp.float32)
        vln_w = jnp.ones((HEADS, 1, HEADC), dtype=jnp.float32)
        vln_b = jnp.zeros((HEADS, 1, HEADC), dtype=jnp.float32)
        W_proj = jax.random.normal(ks[2], (MIDC, MIDC), dtype=jnp.float32) * 0.02
        b_proj = jnp.zeros((MIDC,), dtype=jnp.float32)
        return {'x': x, 'W_qkv': W_qkv, 'b_qkv': b_qkv, 'kln_w': kln_w, 'kln_b': kln_b, 'vln_w': vln_w, 'vln_b': vln_b, 'W_proj': W_proj, 'b_proj': b_proj}
    _L1_attn_all = _L1_attn_setup()
    _L1_attn_in = {k: v for k, v in _L1_attn_all.items() if k in ('W_qkv', 'b_qkv', 'kln_w', 'kln_b', 'vln_w', 'vln_b', 'W_proj', 'b_proj')}
    del _L1_attn_all

    def _L1_ffn_setup():
        import jax, jax.numpy as jnp
        import numpy as np
        TOP_K = 2
        LN_EPS = 1e-05
        key = jax.random.key(seed)
        ks = jax.random.split(key, 8)
        B, S, D, E, H = (16, 256, 64, 8, 256)
        x = jax.random.normal(ks[0], (B, S, D), dtype=jnp.float32)
        Wr = jax.random.normal(ks[1], (D, E), dtype=jnp.float32) * 0.1
        br = jnp.zeros((E,), dtype=jnp.float32)
        ln_g = jnp.ones((E, D), dtype=jnp.float32)
        ln_b = jnp.zeros((E, D), dtype=jnp.float32)
        W1 = jax.random.normal(ks[2], (E, D, H), dtype=jnp.float32) * (1.0 / np.sqrt(D))
        b1 = jnp.zeros((E, H), dtype=jnp.float32)
        W2 = jax.random.normal(ks[3], (E, H, D), dtype=jnp.float32) * (1.0 / np.sqrt(H))
        b2 = jnp.zeros((E, D), dtype=jnp.float32)
        return {'x': x, 'Wr': Wr, 'br': br, 'ln_g': ln_g, 'ln_b': ln_b, 'W1': W1, 'b1': b1, 'W2': W2, 'b2': b2}
    _L1_ffn_all = _L1_ffn_setup()
    _L1_ffn_in = {k: v for k, v in _L1_ffn_all.items() if k in ('Wr', 'br', 'ln_g', 'ln_b', 'W1', 'b1', 'W2', 'b2')}
    del _L1_ffn_all
    return {'x': x, 'L0_conv_ln1_w': _L0_conv_in['ln1_w'], 'L0_conv_ln1_b': _L0_conv_in['ln1_b'], 'L0_conv_qkv_w': _L0_conv_in['qkv_w'], 'L0_conv_qkv_b': _L0_conv_in['qkv_b'], 'L0_conv_rpb_table': _L0_conv_in['rpb_table'], 'L0_conv_proj_w': _L0_conv_in['proj_w'], 'L0_conv_proj_b': _L0_conv_in['proj_b'], 'L0_conv_ln2_w': _L0_conv_in['ln2_w'], 'L0_conv_ln2_b': _L0_conv_in['ln2_b'], 'L0_conv_fc1_w': _L0_conv_in['fc1_w'], 'L0_conv_fc1_b': _L0_conv_in['fc1_b'], 'L0_conv_ln3_w': _L0_conv_in['ln3_w'], 'L0_conv_ln3_b': _L0_conv_in['ln3_b'], 'L0_conv_fc2_w': _L0_conv_in['fc2_w'], 'L0_conv_fc2_b': _L0_conv_in['fc2_b'], 'L0_conv_attn_mask': _L0_conv_in['attn_mask'], 'L0_conv_rel_index': _L0_conv_in['rel_index'], 'L1_attn_W_qkv': _L1_attn_in['W_qkv'], 'L1_attn_b_qkv': _L1_attn_in['b_qkv'], 'L1_attn_kln_w': _L1_attn_in['kln_w'], 'L1_attn_kln_b': _L1_attn_in['kln_b'], 'L1_attn_vln_w': _L1_attn_in['vln_w'], 'L1_attn_vln_b': _L1_attn_in['vln_b'], 'L1_attn_W_proj': _L1_attn_in['W_proj'], 'L1_attn_b_proj': _L1_attn_in['b_proj'], 'L1_ffn_Wr': _L1_ffn_in['Wr'], 'L1_ffn_br': _L1_ffn_in['br'], 'L1_ffn_ln_g': _L1_ffn_in['ln_g'], 'L1_ffn_ln_b': _L1_ffn_in['ln_b'], 'L1_ffn_W1': _L1_ffn_in['W1'], 'L1_ffn_b1': _L1_ffn_in['b1'], 'L1_ffn_W2': _L1_ffn_in['W2'], 'L1_ffn_b2': _L1_ffn_in['b2']}

def reference(x, L0_conv_ln1_w, L0_conv_ln1_b, L0_conv_qkv_w, L0_conv_qkv_b, L0_conv_rpb_table, L0_conv_proj_w, L0_conv_proj_b, L0_conv_ln2_w, L0_conv_ln2_b, L0_conv_fc1_w, L0_conv_fc1_b, L0_conv_ln3_w, L0_conv_ln3_b, L0_conv_fc2_w, L0_conv_fc2_b, L0_conv_attn_mask, L0_conv_rel_index, L1_attn_W_qkv, L1_attn_b_qkv, L1_attn_kln_w, L1_attn_kln_b, L1_attn_vln_w, L1_attn_vln_b, L1_attn_W_proj, L1_attn_b_proj, L1_ffn_Wr, L1_ffn_br, L1_ffn_ln_g, L1_ffn_ln_b, L1_ffn_W1, L1_ffn_b1, L1_ffn_W2, L1_ffn_b2):
    import jax
    import jax.numpy as jnp

    def _L0_conv_ref(x, ln1_w, ln1_b, qkv_w, qkv_b, rpb_table, proj_w, proj_b, ln2_w, ln2_b, fc1_w, fc1_b, ln3_w, ln3_b, fc2_w, fc2_b, attn_mask, rel_index):
        import jax, jax.numpy as jnp
        import numpy as np
        DIM = 64
        HEADS = 8
        HEAD_DIM = DIM // HEADS
        WS = 7
        SHIFT = 3
        H = 56
        W = 56
        B = 32
        WA = WS * WS
        NWH, NWW = (H // WS, W // WS)
        NW = NWH * NWW

        def _make_attn_mask():
            img = np.zeros((H, W), dtype=np.float32)
            cnt = 0
            for hs in (slice(0, -WS), slice(-WS, -SHIFT), slice(-SHIFT, None)):
                for ws_ in (slice(0, -WS), slice(-WS, -SHIFT), slice(-SHIFT, None)):
                    img[hs, ws_] = cnt
                    cnt += 1
            mw = img.reshape(NWH, WS, NWW, WS).transpose(0, 2, 1, 3).reshape(-1, WA)
            diff = mw[:, None, :] - mw[:, :, None]
            return np.where(diff != 0, -100.0, 0.0).astype(np.float32)

        def _make_rel_index():
            coords = np.stack(np.meshgrid(np.arange(WS), np.arange(WS), indexing='ij')).reshape(2, -1)
            rel = coords[:, :, None] - coords[:, None, :]
            rel = rel.transpose(1, 2, 0) + (WS - 1)
            rel[..., 0] *= 2 * WS - 1
            return rel.sum(-1).astype(np.int32)

        def _ln(x, w, b, eps=1e-05):
            m = jnp.mean(x, axis=-1, keepdims=True)
            v = jnp.mean((x - m) ** 2, axis=-1, keepdims=True)
            return (x - m) * jax.lax.rsqrt(v + eps) * w + b
        Bn, Hn, Wn, C = x.shape
        y = _ln(x, ln1_w, ln1_b)
        sh = jnp.roll(y, (-SHIFT, -SHIFT), axis=(1, 2))
        win = sh.reshape(Bn, NWH, WS, NWW, WS, C).transpose(0, 1, 3, 2, 4, 5).reshape(Bn * NW, WA, C)
        qkv = win @ qkv_w.T + qkv_b
        qkv = qkv.reshape(Bn * NW, WA, 3, HEADS, HEAD_DIM).transpose(2, 0, 3, 1, 4)
        q, k, v = (qkv[0], qkv[1], qkv[2])
        scale = HEAD_DIM ** (-0.5)
        attn = jnp.einsum('bhqd,bhkd->bhqk', q * scale, k)
        bias = rpb_table[rel_index]
        attn = attn + jnp.transpose(bias, (2, 0, 1))[None]
        attn = attn.reshape(Bn, NW, HEADS, WA, WA) + attn_mask[None, :, None]
        attn = jax.nn.softmax(attn, axis=-1).reshape(Bn * NW, HEADS, WA, WA)
        out = jnp.einsum('bhqk,bhkd->bhqd', attn, v)
        out = out.transpose(0, 2, 1, 3).reshape(Bn * NW, WA, C)
        out = out @ proj_w.T + proj_b
        out = out.reshape(Bn, NWH, NWW, WS, WS, C).transpose(0, 1, 3, 2, 4, 5).reshape(Bn, Hn, Wn, C)
        out = jnp.roll(out, (SHIFT, SHIFT), axis=(1, 2))
        x = x + out
        z = _ln(x, ln2_w, ln2_b)
        h = jax.nn.gelu(z @ fc1_w.T + fc1_b, approximate=False)
        h = _ln(h, ln3_w, ln3_b)
        x = x + (h @ fc2_w.T + fc2_b)
        return x

    def _L1_attn_ref(x, W_qkv, b_qkv, kln_w, kln_b, vln_w, vln_b, W_proj, b_proj):
        import jax, jax.numpy as jnp
        import numpy as np
        MIDC = 64
        HEADS = 16
        HEADC = MIDC // HEADS
        EPS = 1e-05

        def _layernorm(x, w, b):
            mean = jnp.mean(x, axis=-1, keepdims=True)
            std = jnp.std(x, axis=-1, keepdims=True, ddof=1)
            return w * (x - mean) / (std + EPS) + b
        B, HW, C = x.shape
        bias = x
        qkv = jnp.einsum('bnc,oc->bno', x, W_qkv) + b_qkv
        qkv = qkv.reshape(B, HW, HEADS, 3 * HEADC).transpose(0, 2, 1, 3)
        q, k, v = jnp.split(qkv, 3, axis=-1)
        k = _layernorm(k, kln_w, kln_b)
        v = _layernorm(v, vln_w, vln_b)
        kv = jnp.einsum('bhnd,bhne->bhde', k, v) / HW
        out = jnp.einsum('bhnd,bhde->bhne', q, kv)
        out = out.transpose(0, 2, 1, 3).reshape(B, HW, C)
        ret = out + bias
        proj = jnp.einsum('bnc,oc->bno', ret, W_proj) + b_proj
        return jax.nn.gelu(proj, approximate=False) + bias

    def _L1_ffn_ref(x, Wr, br, ln_g, ln_b, W1, b1, W2, b2):
        import jax, jax.numpy as jnp
        import numpy as np
        TOP_K = 2
        LN_EPS = 1e-05
        B, S, D = x.shape
        N = B * S
        xt = x.reshape(N, D)
        logits = xt @ Wr + br
        probs = jax.nn.softmax(logits, axis=-1)
        top_p, top_idx = jax.lax.top_k(probs, TOP_K)
        weights = top_p / top_p.sum(axis=-1, keepdims=True)
        mu = xt.mean(axis=-1, keepdims=True)
        var = ((xt - mu) ** 2).mean(axis=-1, keepdims=True)
        xn = (xt - mu) * jax.lax.rsqrt(var + LN_EPS)
        xe = xn[None, :, :] * ln_g[:, None, :] + ln_b[:, None, :]
        h = jax.nn.gelu(jnp.einsum('end,edh->enh', xe, W1) + b1[:, None, :], approximate=False)
        y = jnp.einsum('enh,ehd->end', h, W2) + b2[:, None, :]
        y_tok = jnp.transpose(y, (1, 0, 2))
        sel = jnp.take_along_axis(y_tok, top_idx[:, :, None], axis=1)
        out = (weights[:, :, None] * sel).sum(axis=1)
        return out.reshape(B, S, D)

    def _gn(v, G=32, eps=1e-05):
        B_, H_, W_, C_ = v.shape
        g = v.reshape(B_, H_, W_, G, C_ // G)
        m = jnp.mean(g, axis=(1, 2, 4), keepdims=True)
        s = jnp.var(g, axis=(1, 2, 4), keepdims=True)
        return ((g - m) / jnp.sqrt(s + eps)).reshape(v.shape)

    def _ln_c(v, eps=1e-06):
        m = jnp.mean(v, axis=-1, keepdims=True)
        s = jnp.var(v, axis=-1, keepdims=True)
        return (v - m) / jnp.sqrt(s + eps)

    def _ln_t(v, eps=1e-05):
        m = jnp.mean(v, axis=-1, keepdims=True)
        s = jnp.var(v, axis=-1, keepdims=True)
        return (v - m) / jnp.sqrt(s + eps)

    def _to_tokens(v):
        B_, H_, W_, C_ = v.shape
        return v.reshape(B_, H_ * W_, C_)

    def _from_tokens(t, like):
        return t.reshape(like.shape)
    x = _L0_conv_ref(x, L0_conv_ln1_w, L0_conv_ln1_b, L0_conv_qkv_w, L0_conv_qkv_b, L0_conv_rpb_table, L0_conv_proj_w, L0_conv_proj_b, L0_conv_ln2_w, L0_conv_ln2_b, L0_conv_fc1_w, L0_conv_fc1_b, L0_conv_ln3_w, L0_conv_ln3_b, L0_conv_fc2_w, L0_conv_fc2_b, L0_conv_attn_mask, L0_conv_rel_index)
    t = _to_tokens(x)
    t = t + _L1_attn_ref(_ln_t(t), L1_attn_W_qkv, L1_attn_b_qkv, L1_attn_kln_w, L1_attn_kln_b, L1_attn_vln_w, L1_attn_vln_b, L1_attn_W_proj, L1_attn_b_proj)
    t = t + _L1_ffn_ref(_ln_t(t), L1_ffn_Wr, L1_ffn_br, L1_ffn_ln_g, L1_ffn_ln_b, L1_ffn_W1, L1_ffn_b1, L1_ffn_W2, L1_ffn_b2)
    x = _from_tokens(t, x)
    return x

_drawn_inputs = setup_inputs


def setup_inputs(seed=0):
    import zlib

    import numpy as np

    out = dict(_drawn_inputs(seed))
    spreads = {'L0_conv_ln1_w': (1.0, 0.6),
     'L0_conv_ln1_b': (0.0, 0.75),
     'L0_conv_qkv_b': (0.0, 0.273),
     'L0_conv_proj_b': (0.0, 0.1),
     'L0_conv_ln2_w': (1.0, 0.2),
     'L0_conv_ln2_b': (0.0, 0.1),
     'L0_conv_fc1_b': (0.0, 0.1),
     'L0_conv_ln3_w': (1.0, 0.2),
     'L0_conv_ln3_b': (0.0, 0.1),
     'L0_conv_fc2_b': (0.0, 0.1),
     'L1_attn_b_qkv': (0.0, 0.597),
     'L1_attn_kln_w': (1.0, 0.6),
     'L1_attn_kln_b': (0.0, 0.8),
     'L1_attn_vln_w': (1.0, 0.6),
     'L1_attn_vln_b': (0.0, 0.8),
     'L1_attn_b_proj': (0.0, 0.1),
     'L1_ffn_br': (0.0, 0.1),
     'L1_ffn_ln_g': (1.0, 0.2),
     'L1_ffn_ln_b': (0.0, 0.336),
     'L1_ffn_b1': (0.0, 0.333),
     'L1_ffn_b2': (0.0, 0.1)}
    factors = {'L0_conv_qkv_w': 4.244, 'L0_conv_rpb_table': 31.732, 'L1_attn_W_qkv': 5.15}
    for name, (base, spread) in spreads.items():
        noise = np.random.default_rng([zlib.crc32(name.encode()), seed]).standard_normal(out[name].shape)
        drawn = base * np.exp(spread * noise) if base else spread * noise
        out[name] = jnp.asarray(drawn.astype(out[name].dtype))
    for name, factor in factors.items():
        out[name] = (out[name] * factor).astype(out[name].dtype)
    return out
```

```python
from contextlib import ExitStack

import numpy as np

import concourse.bass as bass
from concourse import mybir

F32 = mybir.dt.float32
F16 = mybir.dt.float16
I32 = mybir.dt.int32
ALU = mybir.AluOpType
ACT = mybir.ActivationFunctionType
AX = mybir.AxisListType.X

C = 64
WS = 7
WA = WS * WS
TOK = 2 * WA
GT = 4
GTOK = GT * TOK
HEADS, HD = 8, 8
LH, LD = 16, 4
HID = 256
NE = 8
EPS = 1e-5
SHIFT = 3
XBUF, YBUF = 4, 8
WSCALE = 64.0


def constants():
    p = np.arange(128)
    parts = {
        "ident": np.eye(128),
        "headmask": (p[:, None] % C // HD == np.arange(HEADS)),
        "winblock": (p[:, None] // C == (np.arange(TOK) // WA)[None]),
        "winmask": (p[:, None] // WA == np.arange(2)),
        "parity": np.tile(p[:, None] // WA == np.arange(2), (1, HEADS // 2)),
        "rank": np.tile(NE - np.arange(NE), (128, 1)),
        "row": np.stack([p, p + 128], 1),
        "kvblock": (p[:, None] // LD == (np.arange(C) // LD)[None]),
        "minushalf": np.full((128, GT), -0.5),
        "eps": np.full((128, GT), EPS),
        "tiny": np.full((128, 1), 1e-30),
    }
    at, cols, n = {}, [], 0
    for k, v in parts.items():
        at[k] = (n, n + v.shape[1])
        cols.append(v.astype(np.float32))
        n += v.shape[1]
    return np.ascontiguousarray(np.concatenate(cols, 1)), at


def build(nc, x, cst, wqkv, bqkv, table, projw, projb, fc1w, fc1b, fc2w, fc2b, amask, rel, lnvecs, ln3,
          lwkv, lbkv, lwq, lnkvw, klnb, vlnb, lwp, lbp, wr, br, w1, b1, w2, b2, out):
    IMAGES, _, TILES, _ = x.shape
    GROUPS = TILES // GT
    NPOS = IMAGES and (TILES * TOK)
    TABLE = table.shape[0]
    _, at = constants()

    with ExitStack() as ctx:
        def sb(name, shape, dt=F32):
            return ctx.enter_context(nc.sbuf_tensor(name, shape, dt))

        def sem(name):
            return ctx.enter_context(nc.semaphore(name))

        xg = sb("xg", [TOK, XBUF, GT * C])
        yo = sb("yo", [TOK, YBUF, GT * C])
        tu_img = sb("tu_img", [TOK, TILES * C])
        ut_img = sb("ut_img", [C, TILES * TOK])
        cs = sb("cs", [128, cst.shape[1]])
        bias_ = sb("bias", [128, TILES * HEADS * WA])
        bias = bias_[0:TOK, :].rearrange("p (t c) -> p t c", t=TILES)
        wa = sb("wa", [C + 1, 3 * C])
        wq2 = sb("wq2", [C + 1, 2, C])
        wp = sb("wp", [C + 1, C])
        wf1 = sb("wf1", [C + 1, HID])
        wf2 = sb("wf2", [128, 2, C])
        wkv = sb("wkv", [C + 1, 2 * C])
        wqn = sb("wqn", [C, C + 1])
        lk = sb("lk", [C + 1, C])
        lv = sb("lv", [C + 1, C])
        wlp = sb("wlp", [C, C])
        blp = sb("blp", [C + 1, C])
        i65 = sb("i65", [C, C + 1])
        we1 = [sb(f"we1_{h}", [128, NE * HID], F16) for h in ("hi", "lo")]
        be1 = sb("be1", [128, 2 * NE])
        we2 = sb("we2", [128, NE * 2, C])
        wb2 = sb("wb2", [NE, C])
        wrt = sb("wrt", [C, NE])
        brb = sb("brb", [TOK, NE])
        fc2bias = sb("fc2bias", [TOK, C])
        m65 = sb("m65", [C + 1, C])
        st = {L: sb(f"st{L}", [TOK, GT, 6]) for L in "123ux"}
        mv = {L: sb(f"mv{L}", [TOK, GT, 2]) for L in "123ux"}
        ve = {L: sb(f"ve{L}", [TOK, GT]) for L in "123ux"}
        rs = {L: sb(f"rs{L}", [TOK, GT]) for L in "123ux"}
        z = sb("z", [TOK, GT, C])
        zt = sb("zt", [C + 1, 2 * GT, 2, WA])
        qbd = sb("qbd", [128, GT, TOK])
        kt = sb("kt", [128, GT, WA])
        kexp = sb("kexp", [128, GT, HEADS * WA])
        vexp = sb("vexp", [TOK, 2 * GT, HEADS, HD + 1])
        sc = sb("sc", [TOK, 2, HEADS * WA])
        mx = sb("mx", [TOK, 2, HEADS])
        pr = sb("pr", [TOK, 2, HEADS * WA])
        pt = sb("pt", [TOK, 2, HEADS // 2, TOK])
        rz = sb("rz", [TOK, 2, 4 * HEADS])
        rzm = sb("rzm", [TOK, 2, 4 * HEADS])
        ow = sb("ow", [TOK, 2, 4, C])
        on = sb("on", [TOK, GT, C])
        ot = sb("ot", [C + 1, GTOK])
        x1 = sb("x1", [TOK, GT, C])
        x1b = sb("x1b", [TOK, GT, C])
        z2 = sb("z2", [TOK, GT, C])
        z2t_ = sb("z2t", [C + 1, GTOK])
        hid = sb("hid", [TOK, GT, HID])
        hn = hid
        hnt = sb("hnt", [128, GT, 2, TOK])
        tt = sb("tt", [TOK, GT, C])
        u = sb("u", [TOK, GT, C])
        uts = sb("uts", [C + 1, GTOK])
        kvsq = sb("kvsq", [TOK, GT * 2 * LH, LD])
        kvss = sb("kvss", [TOK, GT * 2 * LH])
        kvln = sb("kvln", [TOK, GT * 2 * LH])
        kvsd = sb("kvsd", [TOK, GT * 2 * LH])
        kvse = sb("kvse", [TOK, GT * 2 * LH])
        kvr = sb("kvr", [TOK, GT * 2 * LH])
        kvn = sb("kvn", [TOK, 2 * GT, C + 1])
        gsum = sb("gsum", [C + 1, C + 1])
        t1s = sb("t1s", [C + 1, C])
        kvb = sb("kvb", [C, C])
        m2 = sb("m2", [C, C + 1])
        utc = sb("utc", [C + 1, GTOK])
        gp = sb("gp", [TOK, GT, C])
        t2 = sb("t2", [TOK, GT, C])
        v3 = sb("v3", [TOK, 6, GT])
        xn = sb("xn", [TOK, GT, 2, C])
        xnt = sb("xnt", [128, GTOK])
        xs = sb("xs", [128, GTOK], F16)
        lg = sb("lg", [TOK, 12, GT, NE])
        lm = sb("lm", [TOK, 8, GT])
        gate = sb("gate", [TOK, GT, NE])
        gtt = sb("gtt", [NE, GTOK])
        gate2 = sb("gate2", [TOK, 2, GT, NE])
        yacc = sb("yacc", [TOK, 2, GT * C])
        ht = sb("ht", [128, 4, GTOK])
        yg = sb("yg", [TOK, 2, GT * C])
        scratch = bias_
        relb = scratch[:, 0:WA * WA].bitcast(I32)
        hot = [scratch[:, WA * WA * h:WA * WA * (h + 1)] for h in (1, 2)]
        pos1, pos = ht[0:WA, 0, :], ht[0:TOK, 1, :]

        ps = [ctx.enter_context(nc.psum_tensor(f"ps{i}", [128, 512], F32)) for i in range(8)]
        pA, pO, pP, pS, pB, pH0, pH1, pY = ps
        pH = [pH0, pH1]

        def k(name):
            a, b = at[name]
            return cs[:, a:b]

        ident = k("ident")

        COUNTS = dict(
            **{f"{s}_{L}": 1 for L in "123ux" for s in ("stats", "meanvar", "vareps", "rstd")},
            z_ready=1, zT_psum=1, zT_ready=1, q_psum=1, q_ready=1, k_psum=1, kT_ready=1, v_psum=1,
            vexp_ready=1, kexp_dve=2, kexp_pool=2, score_psum=4, score_bias=4, score_max=4,
            score_sub=4, prob_ready=2, pT_psum=4, pT_ready=4, o_psum=2, o_recip=2, o_rmask=2,
            o_scaled=2, o_ready=2, oT_psum=1, oT_ready=1, proj_psum=1, x1_ready=1, x1b_ready=1, z2_ready=1,
            z2T_psum=1, z2T_ready=1, fc1_psum=2, hid_ready=2, hn_ready=1, hnT_psum=2,
            hnT_ready=2, fc2_psum=1, t_ready=1, u_ready=1, tu_ready=1, uT_psum=1, uT_ready=1,
            uT_kept=1, kv_psum=1, kv_square=1, kv_ss=1, kv_ln=1, kv_sd=1, kv_se=1, kv_r=1, kv_ready=1,
            g_psum=1, g_ready=1,
            utc_ready=1, lproj_psum=1, gelu_ready=1, t2_ready=1, x_v3=4, x_rstd3=1, x_scale=2, xn_ready=1,
            xnT_psum=1, xnT_ready=1, logit_psum=1, route=20, top_diff=1, tanh_ready=1, gate_ready=1, gate2_ready=1, gateT_psum=1,
            gateT_ready=1, gbias_psum=1, yinit_ready=1,
            xhi_ready=1, xs_ready=1, e1_psum=16, h_ready=16, e2_psum=8, yg_ready=8, y_sum=8,
        )
        S = {name: sem(name) for name in COUNTS}
        x_in, x_out, setup, setup_pos, setup_w1, setup_pe, setup_dve, mix_pe, mix_dve = (sem(n) for n in (
            "x_in", "x_out", "setup", "setup_pos", "setup_w1", "setup_pe", "setup_dve", "mix_pe", "mix_dve"))

        def credit(eng, names):
            for name in names.split():
                eng.sem_inc(S[name], COUNTS[name])

        held = {e: sem(f"held_{e}") for e in ("pe", "dve", "pool", "sp")}

        def now(eng, name, n, t=0, alone=None):
            if isinstance(n, int) and n < 0:
                return
            eng.wait_ge(S[name], COUNTS[name] * (n + 1) + (t + 1))
            if alone:
                eng.sem_inc(held[alone], 1)

        def before(eng, name, n, t=None):
            now(eng, name, n - 1, COUNTS[name] - 1 if t is None else t)

        def spread_keys(eng, t):
            return eng.tensor_tensor(kexp[:, t, :].rearrange("p (h k) -> p h k", k=WA),
                                     kt[:, t, :].unsqueeze(1).to_broadcast([128, HEADS, WA]),
                                     k("headmask").unsqueeze(2).to_broadcast([128, HEADS, WA]), ALU.mult)

        def cols(t):
            return slice(TOK * t, TOK * (t + 1))

        SETUP_LOADS = []

        def load(dst, src):
            SETUP_LOADS.append((dst, src))

        row = slice(C, C + 1)
        w1raw = scratch[:, 3 * WA * WA:3 * WA * WA + NE * HID]
        w1tmp = scratch[:, 3 * WA * WA + NE * HID:3 * WA * WA + 2 * NE * HID]
        load(cs[:, :], cst)
        load(wa[0:C, :], wqkv)
        load(wa[row, :], bqkv)
        load(wp[0:C, :], projw)
        load(wp[row, :], projb)
        load(wf1[0:C, :], fc1w)
        load(wf1[row, :], fc1b)
        load(wf2[:, :, :], fc2w)
        load(wkv[0:C, :], lwkv)
        load(wkv[row, :], lbkv)
        load(wqn[:, :], lwq)
        load(lk[row, :], klnb)
        load(lv[row, :], vlnb)
        load(wlp[:, :], lwp)
        load(blp[row, :], lbp)
        for half in range(2):
            load(w1raw[C * half:C * (half + 1), :], w1)
        load(be1[:, :], b1)
        load(we2[:, :, :], w2)
        load(wb2[:, :], b2)
        load(wrt[:, :], wr)
        load(brb[:, :], br.partition_broadcast(TOK))
        vecs = sb("vecs", [C, 4 + 2 * NE])
        vec3 = sb("vec3", [128, 4])
        kvw = sb("kvw", [C, 2])
        f2row = sb("f2row", [1, C])
        load(vecs[:, :], lnvecs)
        lng2 = sb("lng2", [128, NE])
        for half in range(2):
            load(lng2[C * half:C * (half + 1), :], lnvecs[:, 4:4 + NE])
        load(vec3[:, :], ln3)
        load(kvw[:, :], lnkvw)
        load(f2row[:, :], fc2b)
        load(relb, rel.partition_broadcast(128))
        mask_sb = tu_img[:, 0:TILES * WA]
        for w in range(2):
            load(mask_sb[w * WA:(w + 1) * WA, :].rearrange("q (p k) -> q p k", k=WA),
                 amask.rearrange("(p w) q k -> w q p k", w=2)[w])
        tab = sb("tab", [128, 2, HEADS])
        load(tab[:, 0, :], table[0:128, :])
        load(tab[0:TABLE - 128, 1, :], table[128:TABLE, :])
        ln3bb = sb("ln3bb", [128, 2, TOK])
        ones = sb("ones", [128, TOK])

        block = ctx.enter_context(nc.Block())

        STAGE = {}
        for step in """e split | e ex0 | c gp | a ln1 | c gp2 | a ln1n | a qkv | e ex1 | b z2t | a s0 | a s1 | c gpn |
                       c logit | b fc1 | e ex2 | a v0 | b ln3n | a s2 | a s3 | e ex3 | b hnt | c route | a v1 | b fc2 |
                       e ex4 | b ut | c gates | c gbias | e ex5 | a oT | b kv | e ex6 | a proj | e ex7 | b kvsum |
                       a z2 | e exl""".split("|"):
            stage, name = step.split()
            STAGE[name] = stage
        has = {}

        def images(eng, steps, between):
            def iteration(n, j, stages):
                has.clear()
                has.update(dict.fromkeys(stages, True))
                at_ = dict(a=(n + 1, (j + 1) % GROUPS), b=(n, j), c=(n - GROUPS, j), e=(n - GROUPS - 1, j))
                for name, stage in STAGE.items():
                    if stage in stages and name in steps:
                        steps[name](*at_[stage])

            last = IMAGES - 1
            iteration(-1, -1, "a")
            with eng.Fori(0, GROUPS) as j:
                iteration(j, j, "ab")
            between(0)
            iteration(GROUPS, 0, "abc")
            with eng.Fori(1, GROUPS) as j:
                iteration(GROUPS + j, j, "abce")
            between(1)
            if IMAGES > 3:
                with eng.Fori(2, last) as i:
                    with eng.Fori(0, GROUPS) as j:
                        iteration(i * GROUPS + j, j, "abce")
                    between(i)
            with eng.Fori(0, GROUPS - 1) as j:
                iteration(last * GROUPS + j, j, "abce")
            iteration(IMAGES * GROUPS - 1, GROUPS - 1, "bce")
            between(last)
            with eng.Fori(0, GROUPS) as j:
                iteration(IMAGES * GROUPS + j, j, "ce")
            iteration((IMAGES + 1) * GROUPS, 0, "e")

        @block.sync
        def _(sp):
            sp.sem_inc(x_out, 16 * YBUF)
            for dst, src in SETUP_LOADS:
                sp.dma_start(dst, src).then_inc(setup, 16)

            def load_x(n, i, j):
                if not (isinstance(n, int) and n == 0):
                    sp.wait_ge(x_in, 16 * n)
                    sp.sem_inc(held["sp"], 1)
                now(sp, "x1_ready", n - XBUF, alone="sp")
                sp.dma_start(xg[:, bass.ts(n % XBUF, 1), :],
                             x[bass.ts(i, 1), :, bass.ts(j, GT), :].rearrange("o p t c -> p o (t c)")).then_inc(x_in, 16)

            def store_y(n, i, j):
                now(sp, "y_sum", n, NE - 1, alone="sp")
                sp.wait_ge(x_out, 16 * (n + YBUF))
                sp.sem_inc(held["sp"], 1)
                sp.dma_start(out[bass.ts(i, 1), :, bass.ts(j, GT), :].rearrange("o p t c -> p o (t c)"),
                             yo[:, bass.ts(n % YBUF, 1), :]).then_inc(x_out, 16)

            for j in range(XBUF):
                load_x(j, 0, j)
            sp.wait_ge(setup_dve, 8)
            for w in range(2):
                sp.dma_start(pos[w * WA:(w + 1) * WA, :], pos1).then_inc(setup_pos, 16)
            with sp.Fori(XBUF, GROUPS) as j:
                load_x(j, 0, j)
            with sp.Fori(1, 2) as i:
                with sp.Fori(0, GROUPS) as j:
                    load_x(i * GROUPS + j, i, j)
            with sp.Fori(2, IMAGES) as i:
                with sp.Fori(0, GROUPS) as j:
                    load_x(i * GROUPS + j, i, j)
                    store_y(i * GROUPS + j - 2 * GROUPS, i - 2, j)
            with sp.Fori(IMAGES - 2, IMAGES) as i:
                with sp.Fori(0, GROUPS) as j:
                    store_y(i * GROUPS + j, i, j)
            sp.wait_ge(x_out, 16 * (IMAGES * GROUPS + YBUF))

        @block.tensor
        def _(pe):
            pe.wait_ge(setup, 16 * len(SETUP_LOADS))
            pe.wait_ge(setup_dve, 2)
            pe.matmul(pB[C:C + 1, 0:3 * C], vecs[:, 1:2], wa[0:C, :], start=True, stop=True)
            pe.matmul(pP[C:C + 1, 0:HID], vecs[:, 3:4], wf1[0:C, :], start=True, stop=True).then_inc(setup_pe, 1)
            for b in range(2 * NE):
                pe.matmul(pH0[:, b:b + 1], w1raw[0:C, 128 * b:128 * (b + 1)], vecs[:, 4 + NE + b // 2:5 + NE + b // 2],
                          start=True, stop=True)
            for h in range(2):
                pe.matmul(pA[0:TOK, 0:C], ln3bb[:, h, :], wf2[:, h, :], start=(h == 0), stop=False)
            pe.matmul(pA[0:TOK, 0:C], ones[0:1, :], f2row[:, :], start=False, stop=True).then_inc(setup_pe, 1)
            pe.wait_ge(setup_dve, 4)
            for key in range(WA):
                for half, rows in ((0, 128), (1, TABLE - 128)):
                    at_key = hot[half][0:rows, key:WA * WA:WA]
                    last = pe.matmul(pS[0:WA, key * HEADS:(key + 1) * HEADS], at_key, tab[0:rows, half, :],
                                     start=(half == 0), stop=(half == 1))
            last.then_inc(setup_pe, 1)
            pe.wait_ge(setup_dve, 10)
            credit(pe, "zT_psum q_psum k_psum v_psum score_psum pT_psum o_psum oT_psum proj_psum z2T_psum fc1_psum "
                       "hnT_psum fc2_psum uT_psum kv_psum g_psum lproj_psum xnT_psum logit_psum gateT_psum gbias_psum "
                       "e1_psum e2_psum")

            def transposes(dst, src, signal, width=C):
                for t in range(GT):
                    last = pe.transpose(dst[0:width, cols(t)], src(t), ident[0:TOK, 0:TOK])
                last.then_inc(S[signal], 1)


            def ln1n(a, j):
                now(pe, "g_ready", a - 2)
                now(pe, "z_ready", a, alone="pe")
                transposes(pA, lambda t: z[:, t, :], "zT_psum")

            def qkv(a, j):
                now(pe, "zT_ready", a)
                pe.matmul(pA[:, 0:GTOK], wq2[:, :, :].rearrange("p a b -> p (a b)"), zt[:, :, 0, :],
                          start=True, stop=True).then_inc(S["q_psum"], 1)
                before(pe, "o_scaled", a)
                for w in range(2):
                    last = pe.matmul(pO[C * w:C * (w + 1), 0:GT * WA], wa[:, C:2 * C], zt[:, w:2 * GT:2, 0, :],
                                     start=True, stop=True)
                last.then_inc(S["k_psum"], 1)
                before(pe, "pT_ready", a)
                for t in range(2 * GT):
                    last = pe.matmul(pP[0:TOK, t * C:(t + 1) * C], zt[:, t].rearrange("p a k -> p (a k)"),
                                     wa[:, 2 * C:3 * C], start=True, stop=True)
                last.then_inc(S["v_psum"], 1)

            def score(a, t):
                now(pe, "q_ready", a)
                now(pe, "kexp_pool" if t % 2 else "kexp_dve", a, t // 2)
                now(pe, "score_bias", a - (t == 0), (t - 1) % GT)
                pe.matmul(pS[0:TOK, 0:HEADS * WA], qbd[:, t, :], kexp[:, t, :], start=True, stop=True)\
                    .then_inc(S["score_psum"], 1)

            def attend(a, half):
                now(pe, "prob_ready", a, half)
                if half == 0:
                    now(pe, "vexp_ready", a)
                for t in (2 * half, 2 * half + 1):
                    if t:
                        now(pe, "pT_ready", a, t - 1)
                    for h in range(HEADS // 2):
                        last = pe.transpose(pP[0:TOK, cols(h)], pr[:, t % 2, TOK * h:TOK * (h + 1)], ident[0:TOK, 0:TOK])
                    last.then_inc(S["pT_psum"], 1)
                if half:
                    now(pe, "o_scaled", a, 0)
                else:
                    now(pe, "kT_ready", a)
                for t in (2 * half, 2 * half + 1):
                    now(pe, "pT_ready", a, t)
                    o = pO[0:TOK, (t % 2) * 144:(t % 2 + 1) * 144].rearrange("p (w h d) -> p w h d", w=2, h=HEADS)
                    for h in range(HEADS // 2):
                        last = pe.matmul(o[:, :, 2 * h:2 * h + 2, :], pt[:, t % 2, h, :],
                                         vexp[:, 2 * t:2 * t + 2, 2 * h:2 * h + 2, :], start=True, stop=True)
                last.then_inc(S["o_psum"], 1)

            def oT(a, j):
                if has.get("b"):
                    now(pe, "uT_kept", a - 1)
                else:
                    now(pe, "q_ready", a)
                now(pe, "o_ready", a, 1, alone="pe")
                transposes(pA, lambda t: on[:, t, :], "oT_psum")

            def proj(a, j):
                now(pe, "oT_ready", a)
                for t in range(GT):
                    last = pe.matmul(pA[0:TOK, C * t:C * (t + 1)], ot[:, cols(t)], wp[:, :], start=True, stop=True)
                last.then_inc(S["proj_psum"], 1)

            def z2t(n, j):
                if has.get("a"):
                    now(pe, "q_ready", n + 1)
                else:
                    now(pe, "g_ready", n - 1)
                now(pe, "z2_ready", n, alone="pe")
                transposes(pA, lambda t: z2[:, t, :], "z2T_psum")

            def fc1(n, j):
                if has.get("c"):
                    now(pe, "route", n - GROUPS)
                else:
                    now(pe, "kv_ready", n - 1)
                now(pe, "z2T_ready", n)
                for t in range(GT):
                    last = pe.matmul((pB, pA)[t // 2][0:TOK, (t % 2) * HID:(t % 2 + 1) * HID], z2t_[:, cols(t)], wf1[:, :],
                                     start=True, stop=True)
                    if t % 2:
                        last.then_inc(S["fc1_psum"], 1)

            def hnt_(n, j):
                now(pe, "hn_ready", n)
                for t in range(GT):
                    for h in range(2):
                        last = pe.transpose((pB, pA)[t // 2][:, TOK * (2 * (t % 2) + h):TOK * (2 * (t % 2) + h + 1)],
                                            hn[:, t, 128 * h:128 * (h + 1)], ident[0:TOK, 0:TOK])
                    if t % 2:
                        last.then_inc(S["hnT_psum"], 1)

            def fc2(n, j):
                for t in range(GT):
                    if t % 2 == 0:
                        now(pe, "hnT_ready", n, t // 2)
                    for h in range(2):
                        last = pe.matmul(pB[0:TOK, C * t:C * (t + 1)], hnt[:, t, h, :], wf2[:, h, :],
                                         start=(h == 0), stop=(h == 1))
                last.then_inc(S["fc2_psum"], 1)

            def ut(n, j):
                now(pe, "u_ready", n, alone="pe")
                transposes(pA, lambda t: u[:, t, :], "uT_psum")

            def kv(n, j):
                if has.get("c"):
                    now(pe, "yinit_ready", n - GROUPS)
                now(pe, "uT_ready", n)
                for t in range(GT):
                    last = pe.matmul(pB[0:TOK, 128 * t:128 * (t + 1)], uts[:, cols(t)], wkv[:, :], start=True, stop=True)
                last.then_inc(S["kv_psum"], 1)

            def kvsum(n, j):
                now(pe, "kv_ready", n)
                if has.get("a"):
                    now(pe, "x1_ready", n + 1)
                for t in range(GT):
                    last = pe.matmul(pA[0:C + 1, 0:C + 1], kvn[:, 2 * t, :], kvn[:, 2 * t + 1, :],
                                     start=(t == 0), stop=(t == GT - 1))
                last.then_inc(S["g_psum"], 1)

            def mix(i):
                pe.wait_ge(mix_dve, 5 * i + 1)
                pe.matmul(pA[0:C + 1, 0:C], gsum[:, :], lk[:, :], start=True, stop=True).then_inc(mix_pe, 1)
                pe.wait_ge(mix_dve, 5 * i + 2)
                pe.matmul(pA[0:C, 0:C], t1s[:, :], lv[:, :], start=True, stop=True).then_inc(mix_pe, 1)
                pe.wait_ge(mix_dve, 5 * i + 3)
                pe.sem_inc(held["pe"], 1)
                pe.matmul(pA[0:C, 0:C + 1], kvb[:, :], wqn[:, :], start=True, stop=True).then_inc(mix_pe, 1)
                pe.wait_ge(mix_dve, 5 * i + 4)
                pe.matmul(pA[0:C + 1, 0:C], m2[:, :], wlp[:, :], start=True, stop=True).then_inc(mix_pe, 1)
                pe.wait_ge(mix_dve, 5 * i + 5)

            def gp_(c, j):
                if has.get("b"):
                    now(pe, "kv_ready", c + GROUPS - 1)
                else:
                    now(pe, "yinit_ready", c - 1)
                now(pe, "utc_ready", c)
                for t in range(GT):
                    last = pe.matmul(pB[0:TOK, C * t:C * (t + 1)], utc[:, cols(t)], m65[:, :], start=True, stop=True)
                last.then_inc(S["lproj_psum"], 1)

            def gpn(c, j):
                now(pe, "gelu_ready", c)
                now(pe, "xn_ready", c)
                transposes(pB, lambda t: xn[:, t, :, :].rearrange("p a c -> p (a c)"), "xnT_psum", 2 * C)
                now(pe, "xnT_ready", c)
                pe.sem_inc(held["pe"], 1)
                for t in range(GT):
                    last = pe.matmul(pB[0:TOK, NE * t:NE * (t + 1)], xnt[0:C, cols(t)], wrt[:, :], start=True, stop=True)
                last.then_inc(S["logit_psum"], 1)

            def gates(c, j):
                if has.get("b"):
                    now(pe, "t_ready", c + GROUPS)
                now(pe, "gate_ready", c, alone="pe")
                transposes(pB, lambda t: gate[:, t, :], "gateT_psum", NE)

            def gbias(c, j):
                now(pe, "gateT_ready", c)
                pe.sem_inc(held["pe"], 1)
                for t in range(GT):
                    last = pe.matmul(pB[0:TOK, C * t:C * (t + 1)], gtt[:, cols(t)], wb2[:, :], start=True, stop=True)
                last.then_inc(S["gbias_psum"], 1)

            def expert_in(d, e):
                if e == 0:
                    now(pe, "xs_ready", d)
                for b in (2 * e, 2 * e + 1):
                    now(pe, "h_ready", d - (b < 2), (b - 2) % (2 * NE))
                    for half in range(2):
                        last = pe.matmul(pH[b % 2][:, 0:GTOK], we1[half][:, 128 * b:128 * (b + 1)], xs[:, :],
                                         start=(half == 0), stop=(half == 1))
                    last.then_inc(S["e1_psum"], 1)

            def expert_out(d, e):
                now(pe, "h_ready", d, 2 * e + 1)
                now(pe, "yg_ready", d - (e == 0), (e - 1) % NE)
                for t in range(GT):
                    for h in range(2):
                        last = pe.matmul(pY[0:TOK, C * t:C * (t + 1)], ht[:, 2 * (e % 2) + h, cols(t)], we2[:, 2 * e + h, :],
                                         start=(h == 0), stop=(h == 1))
                last.then_inc(S["e2_psum"], 1)

            def expert(d, e):
                if e < NE:
                    expert_in(d, e)
                if e > 0:
                    expert_out(d, e - 1)

            steps = dict(ln1n=ln1n, qkv=qkv, oT=oT, proj=proj, z2t=z2t, fc1=fc1, hnt=hnt_, fc2=fc2, ut=ut, kv=kv,
                         kvsum=kvsum, gp=gp_, gpn=gpn, gates=gates, gbias=gbias,
                         v0=lambda a, j: attend(a, 0), v1=lambda a, j: attend(a, 1), exl=lambda d, j: expert(d, NE))
            for t in range(GT):
                steps[f"s{t}"] = lambda a, j, t=t: score(a, t)
            for e in range(NE):
                steps[f"ex{e}"] = lambda d, j, e=e: expert(d, e)
            images(pe, steps, mix)

        @block.vector
        def _(ve_):
            dve = ve_
            dve.wait_ge(setup, 16 * len(SETUP_LOADS))
            dve.memset(ones[:, :], 1.0).then_inc(setup_dve, 1)
            dve.wait_ge(setup_dve, 1)
            for h in range(2):
                last = dve.tensor_scalar(ln3bb[:, h, :], ones[:, :], vec3[:, 2 + h:3 + h], None, ALU.mult)
            last.then_inc(setup_dve, 1)
            for h, rows in ((0, 128), (1, TABLE - 128)):
                last = dve.tensor_scalar(hot[h][0:rows, :], relb[0:rows, :], k("row")[0:rows, h:h + 1], None, ALU.is_equal)
            last.then_inc(setup_dve, 2)
            dve.memset(blp[0:C, :], 0.0)
            dve.memset(i65[:, C:C + 1], 0.0)
            dve.tensor_copy(i65[:, 0:C], ident[0:C, 0:C])
            for ones_row in (zt[row], ot[row, :], z2t_[row, :], uts[row, :], utc[row, :]):
                dve.memset(ones_row, 1.0)
            dve.memset(kvn[:, :, C:C + 1], 1.0)
            dve.tensor_copy(vexp[:, :, :, HD], k("parity")[0:TOK].unsqueeze(1).to_broadcast([TOK, 2 * GT, HEADS]))
            dve.memset(gsum[:, :], 0.0)
            dve.tensor_scalar(lk[0:C, :], ident[0:C, 0:C], kvw[:, 0:1], None, ALU.mult)
            dve.tensor_scalar(lv[0:C, :], ident[0:C, 0:C], kvw[:, 1:2], None, ALU.mult)
            dve.tensor_reduce(kvss[0:C + 1, 0:2 * LH], wkv[:, :].rearrange("p (g d) -> p g d", d=LD), AX, ALU.add)\
                .then_inc(setup_dve, 1)
            dve.wait_ge(setup_dve, 5)
            dve.scalar_tensor_tensor(out=wkv[:, :].rearrange("p (g d) -> p g d", d=LD),
                                     in0=kvss[0:C + 1, 0:2 * LH].unsqueeze(2).to_broadcast([C + 1, 2 * LH, LD]),
                                     scalar=-1.0 / LD, in1=wkv[:, :].rearrange("p (g d) -> p g d", d=LD),
                                     op0=ALU.mult, op1=ALU.add)
            dve.wait_ge(setup_pe, 2)
            dve.tensor_tensor(wa[row, :], pB[row, 0:3 * C], wa[row, :], ALU.add)
            dve.tensor_scalar(wa[0:C, :], wa[0:C, :], vecs[:, 0:1], None, ALU.mult)
            dve.tensor_tensor(wf1[row, :], pP[row, 0:HID], wf1[row, :], ALU.add)
            dve.tensor_scalar(wf1[0:C, :], wf1[0:C, :], vecs[:, 2:3], None, ALU.mult)
            dve.tensor_tensor(be1[:, :], pH0[:, 0:2 * NE], be1[:, :], ALU.add)
            for e in range(NE):
                part = slice(e * HID, (e + 1) * HID)
                last = dve.tensor_scalar(w1tmp[:, part], w1raw[:, part], lng2[:, e:e + 1], WSCALE, ALU.mult, ALU.mult)
            last.then_inc(setup_w1, 1)
            dve.wait_ge(setup_w1, 1)
            dve.tensor_copy(we1[0][:, :], w1tmp).then_inc(setup_w1, 1)
            dve.wait_ge(setup_w1, 2)
            dve.tensor_tensor(we1[1][:, :], w1tmp, we1[0][:, :], ALU.subtract).then_inc(setup_w1, 1)
            dve.wait_ge(setup_w1, 3)
            for h in range(2):
                dve.tensor_scalar(wf2[:, h, :], wf2[:, h, :], vec3[:, h:h + 1], None, ALU.mult)
            dve.tensor_copy(fc2bias[:, :], pA[0:TOK, 0:C]).then_inc(setup_dve, 1)
            dve.wait_ge(setup_dve, 6)
            for w in range(2):
                dve.tensor_scalar(wq2[:, w, :], wa[:, 0:C], float(HD) ** -0.5, None, ALU.mult)
            dve.wait_ge(setup_pe, 3)
            dve.tensor_copy(pos1.rearrange("p (h k) -> p h k", k=WA),
                            pS[0:WA, 0:WA * HEADS].rearrange("p (k h) -> p h k", h=HEADS)).then_inc(setup_dve, 2)
            dve.wait_ge(setup_pos, 32)
            for t in range(TILES):
                last = dve.tensor_tensor(bias[:, t, :].rearrange("p (h k) -> p h k", k=WA),
                                         pos.rearrange("p (h k) -> p h k", k=WA),
                                         mask_sb[:, t * WA:(t + 1) * WA].unsqueeze(1).to_broadcast([TOK, HEADS, WA]), ALU.add)
            last.then_inc(setup_dve, 2)
            dve.wait_ge(setup_dve, 10)
            credit(dve, "stats_1 stats_2 stats_3 stats_u stats_x meanvar_1 meanvar_2 meanvar_3 meanvar_u meanvar_x z_ready "
                        "q_ready vexp_ready kexp_dve score_bias score_max o_recip o_rmask o_scaled o_ready "
                        "x1_ready z2_ready hn_ready t_ready u_ready kv_ss kv_se kv_r kv_ready g_ready utc_ready t2_ready "
                        "xn_ready route top_diff gate_ready gate2_ready yg_ready yinit_ready xhi_ready xs_ready")

            def statistics(n, L, tiles):
                for t in range(GT):
                    if L == "3" and t % 2 == 0:
                        now(dve, "hid_ready", n, t // 2)
                    last = dve.bn_stats(st[L][:, t, :], tiles(t))
                last.then_inc(S[f"stats_{L}"], 1)
                now(dve, f"stats_{L}", n, alone="dve")
                for t in range(GT):
                    last = dve.bn_aggr(mv[L][:, t, :], st[L][:, t, :])
                last.then_inc(S[f"meanvar_{L}"], 1)

            def normalize(n, L, dst, tiles, signal):
                now(dve, f"rstd_{L}", n)
                for t in range(GT):
                    last = dve.tensor_scalar(dst[:, t, :], tiles(t), mv[L][:, t, 0:1], rs[L][:, t:t + 1],
                                             ALU.subtract, ALU.mult)
                last.then_inc(S[signal], 1)

            def x_tile(n, t):
                return xg[:, bass.ts(n % XBUF, 1), C * t:C * (t + 1)].rearrange("p a c -> p (a c)")

            def ln1(a, j):
                dve.wait_ge(x_in, 16 * (a + 1))
                statistics(a, "1", lambda t: x_tile(a, t))

            def ln1n(a, j):
                before(dve, "zT_psum", a)
                normalize(a, "1", z, lambda t: x_tile(a, t), "z_ready")

            def qkv(a, j):
                now(dve, "q_psum", a)
                before(dve, "score_psum", a)
                dve.tensor_tensor(qbd[:, :, :], pA[:, 0:GTOK].rearrange("p (t c) -> p t c", c=TOK),
                                  k("winblock").unsqueeze(1).to_broadcast([128, GT, TOK]), ALU.mult)\
                    .then_inc(S["q_ready"], 1)
                now(dve, "kT_ready", a)
                spread_keys(dve, 0).then_inc(S["kexp_dve"], 1)
                now(dve, "v_psum", a)
                before(dve, "o_psum", a)
                dve.tensor_tensor(vexp[:, :, :, 0:HD], pP[0:TOK, :].rearrange("p (t h d) -> p t h d", h=HEADS, d=HD),
                                  k("parity")[0:TOK].unsqueeze(1).unsqueeze(3).to_broadcast([TOK, 2 * GT, HEADS, HD]),
                                  ALU.mult).then_inc(S["vexp_ready"], 1)
                spread_keys(dve, 2).then_inc(S["kexp_dve"], 1)

            def softmax_max(a, j, t):
                now(dve, "score_psum", a, t)
                now(dve, "prob_ready", a - (t < 2), 1 - t // 2)
                dve.tensor_tensor(sc[:, t % 2, :], pS[0:TOK, 0:HEADS * WA],
                                  bias[:, bass.ds(j * GT + t, 1), :].rearrange("p a b -> p (a b)"), ALU.add)\
                    .then_inc(S["score_bias"], 1)
                now(dve, "score_bias", a, t)
                dve.tensor_reduce(mx[:, t % 2, :], sc[:, t % 2, :].rearrange("p (h k) -> p h k", k=WA), AX, ALU.max)\
                    .then_inc(S["score_max"], 1)

            def heads_out(n, half):
                now(dve, "o_psum", n, half)
                o = pO[0:TOK, 0:288].rearrange("p (t h d) -> p t h d", t=4, d=HD + 1)
                dve.reciprocal(rz[:, half, :].rearrange("p (t h) -> p t h", h=HEADS), o[:, :, :, HD]).then_inc(S["o_recip"], 1)
                now(dve, "o_recip", n, half)
                dve.tensor_tensor(rzm[:, half, :].rearrange("p (t w h) -> p t w h", t=2, w=2),
                                  rz[:, half, :].rearrange("p (t w h) -> p t w h", t=2, w=2),
                                  k("winmask")[0:TOK].unsqueeze(1).unsqueeze(3).to_broadcast([TOK, 2, 2, HEADS]),
                                  ALU.mult).then_inc(S["o_rmask"], 1)
                now(dve, "o_rmask", n, half)
                dve.tensor_tensor(ow[:, half].rearrange("p t (h d) -> p t h d", d=HD), o[:, :, :, 0:HD],
                                  rzm[:, half, :].rearrange("p (t h) -> p t h", h=HEADS).unsqueeze(3)
                                  .to_broadcast([TOK, 4, HEADS, HD]), ALU.mult).then_inc(S["o_scaled"], 1)
                now(dve, "o_scaled", n, half)
                if half == 0:
                    before(dve, "oT_psum", n)
                pair = ow[:, half].rearrange("p (t w) c -> p t w c", w=2)
                dve.tensor_tensor(on[:, 2 * half:2 * half + 2, :], pair[:, :, 0], pair[:, :, 1], ALU.add)\
                    .then_inc(S["o_ready"], 1)

            def proj(a, j):
                now(dve, "proj_psum", a)
                before(dve, "x1b_ready", a)
                dve.tensor_tensor(x1[:, :, :], pA[0:TOK, 0:GT * C].rearrange("p (t c) -> p t c", c=C),
                                  xg[:, bass.ts(a % XBUF, 1), :].rearrange("p a (t c) -> p (a t) c", c=C), ALU.add)\
                    .then_inc(S["x1_ready"], 1)
                now(dve, "x1_ready", a)
                statistics(a, "2", lambda t: x1[:, t, :])

            def z2n(a, j):
                before(dve, "z2T_psum", a)
                normalize(a, "2", z2, lambda t: x1[:, t, :], "z2_ready")

            def fc1(n, j):
                statistics(n, "3", lambda t: hid[:, t, :])

            def ln3n(n, j):
                normalize(n, "3", hn, lambda t: hid[:, t, :], "hn_ready")

            def fc2(n, j):
                now(dve, "fc2_psum", n)
                now(dve, "x1b_ready", n)
                before(dve, "tu_ready", n)
                dve.tensor_tensor(tt[:, :, :], pB[0:TOK, 0:GT * C].rearrange("p (t c) -> p t c", c=C),
                                  x1b[:, :, :], ALU.add).then_inc(S["t_ready"], 1)
                now(dve, "t_ready", n)
                statistics(n, "u", lambda t: tt[:, t, :])

            def ut(n, j):
                before(dve, "uT_psum", n)
                normalize(n, "u", u, lambda t: tt[:, t, :], "u_ready")

            def kv(n, j):
                now(dve, "kv_square", n)
                dve.tensor_reduce(kvss[:, :], kvsq[:, :, :], AX, ALU.add).then_inc(S["kv_ss"], 1)

            def kvsum(n, j):
                now(dve, "kv_sd", n)
                dve.tensor_scalar(kvse[:, :], kvsd[:, :], EPS, None, ALU.add).then_inc(S["kv_se"], 1)
                now(dve, "kv_se", n)
                dve.reciprocal(kvr[:, :], kvse[:, :]).then_inc(S["kv_r"], 1)
                now(dve, "kv_r", n)
                before(dve, "g_psum", n)
                dve.tensor_tensor(kvn[:, :, 0:C].rearrange("p t (h d) -> p t h d", d=LD),
                                  pB[0:TOK, :].rearrange("p (t h d) -> p t h d", h=LH, d=LD),
                                  kvr[:, :].rearrange("p (t h) -> p t h", h=LH).unsqueeze(3)
                                  .to_broadcast([TOK, 2 * GT, LH, LD]), ALU.mult).then_inc(S["kv_ready"], 1)
                now(dve, "g_psum", n)
                before(dve, "g_ready", n)
                dve.tensor_tensor(gsum[:, :], pA[0:C + 1, 0:C + 1], gsum[:, :], ALU.add).then_inc(S["g_ready"], 1)

            def mix(i):
                now(dve, "g_ready", (i + 1) * GROUPS - 1)
                dve.sem_inc(mix_dve, 1)
                dve.wait_ge(mix_pe, 4 * i + 1)
                dve.tensor_copy(t1s[:, :], pA[0:C + 1, 0:C]).then_inc(mix_dve, 1)
                dve.memset(gsum[:, :], 0.0)
                dve.wait_ge(mix_pe, 4 * i + 2)
                dve.tensor_tensor(kvb[:, :], pA[0:C, 0:C], k("kvblock")[0:C, :], ALU.mult).then_inc(mix_dve, 1)
                dve.wait_ge(mix_pe, 4 * i + 3)
                dve.scalar_tensor_tensor(out=m2[:, :], in0=pA[0:C, 0:C + 1], scalar=1.0 / NPOS, in1=i65[:, :],
                                         op0=ALU.mult, op1=ALU.add).then_inc(mix_dve, 1)
                dve.wait_ge(mix_pe, 4 * i + 4)
                now(dve, "lproj_psum", (i - 1) * GROUPS - 1)
                dve.tensor_tensor(m65[:, :], pA[0:C + 1, 0:C], blp[:, :], ALU.add).then_inc(mix_dve, 1)
                dve.wait_ge(mix_dve, 5 * i + 5)

            def gp_(c, j):
                before(dve, "lproj_psum", c)
                now(dve, "uT_kept", c)
                dve.tensor_copy(utc[0:C, :], ut_img[:, bass.ds(j * GTOK, GTOK)]).then_inc(S["utc_ready"], 1)

            def gp2(c, j):
                now(dve, "gelu_ready", c)
                now(dve, "tu_ready", c)
                before(dve, "yinit_ready", c)
                dve.tensor_tensor(t2[:, :, :].rearrange("p t c -> p (t c)"), gp[:, :, :].rearrange("p t c -> p (t c)"),
                                  tu_img[:, bass.ds(j * (GT * C), GT * C)], ALU.add).then_inc(S["t2_ready"], 1)
                now(dve, "t2_ready", c)
                statistics(c, "x", lambda t: t2[:, t, :])

            def gpn(c, j):
                now(dve, "x_scale", c, 0)
                before(dve, "xnT_psum", c)
                for t in range(GT):
                    last = dve.tensor_scalar(xn[:, t, :, :], t2[:, t, :].unsqueeze(1).to_broadcast([TOK, 2, C]),
                                             mv["x"][:, t, 0:1], v3[:, 4, t:t + 1], ALU.subtract, ALU.mult)
                last.then_inc(S["xn_ready"], 1)

            def logit(c, j):
                now(dve, "logit_psum", c)
                now(dve, "x_scale", c, 1)
                dve.tensor_tensor(lg[:, 0], pB[0:TOK, 0:GT * NE].rearrange("p (t e) -> p t e", e=NE),
                                  v3[:, 5, :].unsqueeze(2).to_broadcast([TOK, GT, NE]), ALU.mult).then_inc(S["route"], 1)

            def route(c, j):
                done = [1]

                def step(ins):
                    ins.then_inc(S["route"], 1)
                    now(dve, "route", c, done[0])
                    done[0] += 1

                def wide(v):
                    return v.unsqueeze(2).to_broadcast([TOK, GT, NE])

                now(dve, "route", c, 0)
                L, M = (lambda a: lg[:, a]), (lambda a: lm[:, a])
                rank = k("rank")[0:TOK].unsqueeze(1).to_broadcast([TOK, GT, NE])
                step(dve.tensor_tensor(L(1), L(0), brb[:, :].unsqueeze(1).to_broadcast([TOK, GT, NE]), ALU.add))
                for half, src in ((0, L(1)), (1, L(5))):
                    a = 2 + 4 * half
                    step(dve.tensor_reduce(M(2 * half), src, AX, ALU.max))
                    step(dve.tensor_tensor(L(a), src, wide(M(2 * half)), ALU.is_equal))
                    step(dve.tensor_tensor(L(a + 1), L(a), rank, ALU.mult))
                    step(dve.tensor_reduce(M(2 * half + 1), L(a + 1), AX, ALU.max))
                    step(dve.tensor_tensor(L(a + 2), L(a + 1), wide(M(2 * half + 1)), ALU.is_equal))
                    if half == 0:
                        step(dve.scalar_tensor_tensor(out=L(5), in0=L(4), scalar=-1e30, in1=L(1), op0=ALU.mult, op1=ALU.add))
                dve.tensor_tensor(M(4), M(2), M(0), ALU.subtract).then_inc(S["top_diff"], 1)
                dve.sem_inc(S["route"], COUNTS["route"] - done[0] - 4)

            def gates(c, j):
                L, M = (lambda a: lg[:, a]), (lambda a: lm[:, a])
                now(dve, "tanh_ready", c)
                first = COUNTS["route"] - 4
                dve.tensor_scalar(M(6), M(5), -0.5, 0.5, ALU.mult, ALU.add).then_inc(S["route"], 1)
                dve.tensor_scalar(M(7), M(5), 0.5, 0.5, ALU.mult, ALU.add).then_inc(S["route"], 1)
                now(dve, "route", c, first + 1)
                dve.tensor_tensor(L(9), L(4), M(6).unsqueeze(2).to_broadcast([TOK, GT, NE]), ALU.mult).then_inc(S["route"], 1)
                dve.tensor_tensor(L(10), L(8), M(7).unsqueeze(2).to_broadcast([TOK, GT, NE]), ALU.mult).then_inc(S["route"], 1)
                now(dve, "route", c, first + 3)
                before(dve, "gateT_psum", c)
                dve.tensor_tensor(gate[:, :, :], L(9), L(10), ALU.add).then_inc(S["gate_ready"], 1)
                dve.tensor_tensor(gate2[:, bass.ts(c % 2, 1)].rearrange("p a t e -> p (a t) e"), L(9), L(10), ALU.add)\
                    .then_inc(S["gate2_ready"], 1)

            def gbias(c, j):
                now(dve, "gbias_psum", c)
                now(dve, "y_sum", c - 2, NE - 1)
                dve.tensor_tensor(yacc[:, bass.ts(c % 2, 1), :].rearrange("p a (t c) -> p (a t) c", c=C),
                                  pB[0:TOK, 0:GT * C].rearrange("p (t c) -> p t c", c=C),
                                  t2[:, :, :], ALU.add).then_inc(S["yinit_ready"], 1)

            def split(d, j):
                now(dve, "xnT_ready", d)
                before(dve, "e1_psum", d)
                dve.tensor_copy(xs[:, :], xnt[:, :]).then_inc(S["xhi_ready"], 1)
                now(dve, "xhi_ready", d)
                dve.tensor_tensor(xs[C:2 * C, :], xnt[C:2 * C, :], xs[C:2 * C, :], ALU.subtract).then_inc(S["xs_ready"], 1)

            def expert(d, e):
                if e == 0:
                    now(dve, "gate2_ready", d)
                now(dve, "e2_psum", d, e)
                now(dve, "y_sum", d - (e < 2), (e - 2) % NE)
                dve.tensor_tensor(yg[:, e % 2, :].rearrange("p (t c) -> p t c", c=C),
                                  pY[0:TOK, 0:GT * C].rearrange("p (t c) -> p t c", c=C),
                                  gate2[:, bass.ts(d % 2, 1), :, e:e + 1].rearrange("p a t e -> p (a t) e")
                                  .to_broadcast([TOK, GT, C]), ALU.mult).then_inc(S["yg_ready"], 1)

            steps = dict(ln1=ln1, ln1n=ln1n, qkv=qkv, proj=proj, z2=z2n, fc1=fc1, ln3n=ln3n, fc2=fc2, ut=ut, kv=kv,
                         kvsum=kvsum, gp=gp_, gp2=gp2, gpn=gpn, logit=logit, route=route, gates=gates, gbias=gbias, split=split,
                         v0=lambda a, j: heads_out(a, 0), v1=lambda a, j: heads_out(a, 1),
                         exl=lambda d, j: expert(d, NE - 1))
            for t in range(GT):
                steps[f"s{t}"] = lambda a, j, t=t: softmax_max(a, j, t)
            for e in range(1, NE):
                steps[f"ex{e}"] = lambda d, j, e=e: expert(d, e - 1)
            images(dve, steps, mix)

        @block.gpsimd
        def _(pool):
            pool.wait_ge(setup_dve, 10)
            credit(pool, "vareps_1 vareps_2 vareps_3 vareps_u vareps_x rstd_1 rstd_2 rstd_3 rstd_u rstd_x kexp_pool "
                         "score_sub x1b_ready tu_ready x_v3 x_rstd3 x_scale y_sum")

            def rstd(n, L):
                now(pool, f"meanvar_{L}", n)
                pool.tensor_tensor(ve[L][:, :], mv[L][:, :, 1], k("eps")[0:TOK], ALU.add).then_inc(S[f"vareps_{L}"], 1)
                now(pool, f"vareps_{L}", n)
                pool.tensor_tensor(rs[L][:, :], ve[L][:, :], k("minushalf")[0:TOK], ALU.pow).then_inc(S[f"rstd_{L}"], 1)

            def ln1(a, j):
                before(pool, "z_ready", a)
                rstd(a, "1")

            def qkv(a, j):
                now(pool, "kT_ready", a)
                before(pool, "score_psum", a)
                for t in (1, 3):
                    spread_keys(pool, t).then_inc(S["kexp_pool"], 1)

            def subtract(a, t):
                now(pool, "score_max", a, t)
                s = sc[:, t % 2, :].rearrange("p (h k) -> p h k", k=WA)
                pool.tensor_tensor(s, s, mx[:, t % 2, :].unsqueeze(2).to_broadcast([TOK, HEADS, WA]), ALU.subtract)\
                    .then_inc(S["score_sub"], 1)

            def proj(a, j):
                before(pool, "z2_ready", a)
                rstd(a, "2")
                before(pool, "t_ready", a)
                pool.tensor_tensor(x1b[:, :, :], x1[:, :, :], fc2bias[:, :].unsqueeze(1).to_broadcast([TOK, GT, C]), ALU.add)\
                    .then_inc(S["x1b_ready"], 1)

            def fc1(n, j):
                before(pool, "hn_ready", n)
                rstd(n, "3")

            def fc2(n, j):
                before(pool, "u_ready", n)
                rstd(n, "u")

            def ut(n, j):
                now(pool, "u_ready", n)
                if has.get("c"):
                    now(pool, "t2_ready", n - GROUPS)
                pool.sem_inc(held["pool"], 1)
                pool.tensor_tensor(tu_img[:, bass.ds(j * (GT * C), GT * C)],
                                   tt[:, :, :].rearrange("p t c -> p (t c)"), u[:, :, :].rearrange("p t c -> p (t c)"),
                                   ALU.add).then_inc(S["tu_ready"], 1)

            def gp2(c, j):
                before(pool, "xn_ready", c)
                before(pool, "route", c)
                rstd(c, "x")
                r = rs["x"][:, :]
                now(pool, "rstd_x", c)
                pool.tensor_tensor(v3[:, 0, :], mv["x"][:, :, 1], r, ALU.mult).then_inc(S["x_v3"], 1)
                now(pool, "x_v3", c, 0)
                pool.tensor_tensor(v3[:, 1, :], v3[:, 0, :], r, ALU.mult).then_inc(S["x_v3"], 1)
                now(pool, "x_v3", c, 1)
                pool.tensor_tensor(v3[:, 2, :], v3[:, 1, :], k("eps")[0:TOK], ALU.add).then_inc(S["x_v3"], 2)
                now(pool, "x_v3", c, 3)
                pool.tensor_tensor(v3[:, 3, :], v3[:, 2, :], k("minushalf")[0:TOK], ALU.pow).then_inc(S["x_rstd3"], 1)
                now(pool, "x_rstd3", c)
                pool.tensor_tensor(v3[:, 4, :], v3[:, 3, :], r, ALU.mult).then_inc(S["x_scale"], 1)
                pool.tensor_tensor(v3[:, 5, :], v3[:, 3, :], v3[:, 2, :], ALU.mult).then_inc(S["x_scale"], 1)

            def expert(d, e):
                if e == 0:
                    now(pool, "yinit_ready", d)
                else:
                    now(pool, "y_sum", d, e - 1)
                now(pool, "yg_ready", d, e)
                acc = yacc[:, bass.ts(d % 2, 1), :]
                dst = acc
                if e == NE - 1:
                    pool.wait_ge(x_out, 16 * (d + 1))
                    dst = yo[:, bass.ts(d % YBUF, 1), :]
                pool.sem_inc(held["pool"], 1)
                pool.tensor_tensor(dst, acc, yg[:, e % 2:e % 2 + 1, :], ALU.add).then_inc(S["y_sum"], 1)

            steps = dict(ln1=ln1, qkv=qkv, proj=proj, fc1=fc1, fc2=fc2, ut=ut, gp2=gp2, exl=lambda d, j: expert(d, NE - 1))
            for t in range(GT):
                steps[f"s{t}"] = lambda a, j, t=t: subtract(a, t)
            for e in range(1, NE):
                steps[f"ex{e}"] = lambda d, j, e=e: expert(d, e - 1)
            images(pool, steps, lambda i: None)

        @block.scalar
        def _(act):
            act.wait_ge(setup_dve, 10)
            credit(act, "zT_ready kT_ready prob_ready pT_ready oT_ready z2T_ready hid_ready hnT_ready uT_ready uT_kept "
                        "kv_square kv_ln kv_sd gelu_ready xnT_ready tanh_ready gateT_ready h_ready")

            def copy(dst, src, signal):
                act.activation(dst, src, ACT.Copy).then_inc(S[signal], 1)

            def ln1n(a, j):
                now(act, "zT_psum", a)
                before(act, "v_psum", a)
                copy(zt[0:C], pA[0:C, 0:GTOK].rearrange("p (a k) -> p a k", k=WA).unsqueeze(2)
                     .to_broadcast([C, 2 * GT, 2, WA]), "zT_ready")

            def qkv(a, j):
                now(act, "k_psum", a)
                before(act, "kexp_dve", a)
                before(act, "kexp_pool", a)
                copy(kt[:, :, :].rearrange("p t k -> p (t k)"), pO[:, 0:GT * WA], "kT_ready")

            def softmax_exp(a, half):
                now(act, "score_sub", a, 2 * half + 1)
                now(act, "pT_psum", a - (half == 0), 1 + 2 * (1 - half))
                act.activation(pr[:, :, :].rearrange("p t c -> p (t c)"), sc[:, :, :].rearrange("p t c -> p (t c)"), ACT.Exp)\
                    .then_inc(S["prob_ready"], 1)

            def keep_pt(a, half):
                now(act, "o_psum", a - (half == 0), 1 - half)
                for t in (2 * half, 2 * half + 1):
                    now(act, "pT_psum", a, t)
                    copy(pt[:, t % 2].rearrange("p a c -> p (a c)"), pP[0:TOK, 0:GTOK], "pT_ready")

            def oT(a, j):
                now(act, "oT_psum", a)
                before(act, "proj_psum", a)
                copy(ot[0:C, :], pA[0:C, 0:GTOK], "oT_ready")

            def z2t(n, j):
                now(act, "z2T_psum", n)
                before(act, "fc1_psum", n)
                copy(z2t_[0:C, :], pA[0:C, 0:GTOK], "z2T_ready")

            def fc1(n, j):
                before(act, "hnT_psum", n)
                for half in range(2):
                    now(act, "fc1_psum", n, half)
                    act.activation(hid[:, 2 * half:2 * half + 2, :].rearrange("p t c -> p (t c)"), (pB, pA)[half][0:TOK, :],
                                   ACT.Gelu).then_inc(S["hid_ready"], 1)

            def hnt_(n, j):
                before(act, "fc2_psum", n)
                for half in range(2):
                    now(act, "hnT_psum", n, half)
                    copy(hnt[:, 2 * half:2 * half + 2].rearrange("p t h c -> p (t h c)"), (pB, pA)[half][:, 0:GTOK], "hnT_ready")

            def ut(n, j):
                now(act, "uT_psum", n)
                before(act, "kv_psum", n)
                copy(uts[0:C, :], pA[0:C, 0:GTOK], "uT_ready")
                if has.get("c"):
                    now(act, "utc_ready", n - GROUPS)
                copy(ut_img[:, bass.ds(j * GTOK, GTOK)], pA[0:C, 0:GTOK], "uT_kept")

            def kv(n, j):
                now(act, "kv_psum", n)
                before(act, "kv_ss", n)
                act.activation(kvsq[:, :, :].rearrange("p g d -> p (g d)"), pB[0:TOK, :], ACT.Square).then_inc(S["kv_square"], 1)
                now(act, "kv_ss", n)
                act.activation(kvln[:, :], kvss[:, :], ACT.Ln, bias=k("tiny")[0:TOK], scale=1.0 / (LD - 1)).then_inc(S["kv_ln"], 1)
                now(act, "kv_ln", n)
                before(act, "kv_se", n)
                act.activation(kvsd[:, :], kvln[:, :], ACT.Exp, scale=0.5).then_inc(S["kv_sd"], 1)

            def gp_(c, j):
                now(act, "lproj_psum", c)
                before(act, "t2_ready", c)
                act.activation(gp[:, :, :].rearrange("p t c -> p (t c)"), pB[0:TOK, 0:GT * C], ACT.Gelu).then_inc(S["gelu_ready"], 1)

            def gpn(c, j):
                now(act, "xnT_psum", c)
                before(act, "logit_psum", c)
                before(act, "xs_ready", c)
                copy(xnt[:, :], pB[:, 0:GTOK], "xnT_ready")

            def route(c, j):
                now(act, "top_diff", c)
                act.activation(lm[:, 5, :], lm[:, 4, :], ACT.Tanh, scale=0.5).then_inc(S["tanh_ready"], 1)

            def gates(c, j):
                now(act, "gateT_psum", c)
                before(act, "gbias_psum", c)
                copy(gtt[:, :], pB[0:NE, 0:GTOK], "gateT_ready")

            def expert(d, e):
                now(act, "e2_psum", d - (e < 2), (e - 2) % NE)
                for b in (2 * e, 2 * e + 1):
                    now(act, "e1_psum", d, b)
                    act.activation(ht[:, b % 4, :], pH[b % 2][:, 0:GTOK], ACT.Gelu, bias=be1[:, b:b + 1],
                                   scale=1.0 / WSCALE).then_inc(S["h_ready"], 1)

            def both(f, g):
                return lambda a, j: (f(a, j), g(a, j))

            steps = dict(ln1n=ln1n, qkv=qkv, oT=oT, z2t=z2t, fc1=fc1, hnt=hnt_, ut=ut, kv=kv, gp=gp_, gpn=gpn,
                         route=route, gates=gates, s1=lambda a, j: softmax_exp(a, 0), s3=lambda a, j: softmax_exp(a, 1),
                         v0=lambda a, j: keep_pt(a, 0), v1=lambda a, j: keep_pt(a, 1))
            for e in range(NE):
                steps[f"ex{e}"] = lambda d, j, e=e: expert(d, e)
            images(act, steps, lambda i: None)


def layout(inputs):
    x = np.asarray(inputs["x"])
    B, H, W, _ = x.shape
    NW = H // WS
    v = {k: np.asarray(a) for k, a in inputs.items()}
    win = np.roll(x, (-SHIFT, -SHIFT), axis=(1, 2)).reshape(B, NW, WS, NW, WS, C).transpose(0, 1, 3, 2, 4, 5)
    win = win.reshape(B, NW * NW // 2, TOK, C).transpose(0, 2, 1, 3)
    lw = v["L1_attn_W_qkv"].reshape(LH, 3, LD, C).transpose(1, 0, 2, 3).reshape(3, C, C)
    lb = v["L1_attn_b_qkv"].reshape(LH, 3, LD).transpose(1, 0, 2).reshape(3, C)
    col = lambda a: a.reshape(-1, 1)
    line = lambda a: a.reshape(1, -1)
    halves = lambda a: a.reshape(2, 128, -1).transpose(1, 0, 2)
    p0, p1, p2 = "L0_conv_", "L1_attn_", "L1_ffn_"
    return dict(
        x=win, cst=constants()[0],
        wqkv=v[p0 + "qkv_w"].T, bqkv=line(v[p0 + "qkv_b"]),
        table=v[p0 + "rpb_table"], projw=v[p0 + "proj_w"].T, projb=line(v[p0 + "proj_b"]),
        fc1w=v[p0 + "fc1_w"].T, fc1b=line(v[p0 + "fc1_b"]), fc2w=halves(v[p0 + "fc2_w"].T), fc2b=line(v[p0 + "fc2_b"]),
        amask=v[p0 + "attn_mask"], rel=v[p0 + "rel_index"].reshape(-1),
        lnvecs=np.concatenate([col(v[p0 + a]) for a in ("ln1_w", "ln1_b", "ln2_w", "ln2_b")]
                              + [v[p2 + "ln_g"].T, v[p2 + "ln_b"].T], 1),
        ln3=np.concatenate([v[p0 + a].reshape(2, 128).T for a in ("ln3_w", "ln3_b")], 1),
        lwkv=np.concatenate([lw[1].T, lw[2].T], 1), lbkv=line(np.concatenate([lb[1], lb[2]])),
        lwq=np.concatenate([lw[0], col(lb[0])], 1),
        lnkvw=np.concatenate([col(v[p1 + "kln_w"]), col(v[p1 + "vln_w"])], 1),
        klnb=line(v[p1 + "kln_b"]), vlnb=line(v[p1 + "vln_b"]),
        lwp=v[p1 + "W_proj"].T, lbp=line(v[p1 + "b_proj"]),
        wr=v[p2 + "Wr"], br=v[p2 + "br"],
        w1=v[p2 + "W1"].transpose(1, 0, 2).reshape(C, NE * HID), b1=v[p2 + "b1"].reshape(2 * NE, 128).T,
        w2=v[p2 + "W2"].reshape(NE, 2, 128, C).transpose(2, 0, 1, 3).reshape(128, NE * 2, C), b2=v[p2 + "b2"],
    )


def kernel(**inputs):
    import concourse.bacc as bacc
    from concourse.bass_utils import run_bass_kernel_spmd

    B, H, W, _ = inputs["x"].shape
    nc = bacc.Bacc("TRN2", target_bir_lowering=False, num_devices=1)
    arrays, args = {}, []
    for name, a in layout(inputs).items():
        a = np.ascontiguousarray(a)
        arrays[f"in_{name}"] = a
        args.append(nc.dram_tensor(f"in_{name}", a.shape, mybir.dt.from_np(a.dtype), kind="ExternalInput").ap())
    shape = arrays["in_x"].shape
    args.append(nc.dram_tensor("out_y", shape, F32, kind="ExternalOutput").ap())
    build(nc, *args)
    r = run_bass_kernel_spmd(nc, [arrays], core_ids=[0])
    y = r.results[0]["out_y"]
    NW = H // WS
    y = y.transpose(0, 2, 1, 3).reshape(B, NW, NW, WS, WS, C).transpose(0, 1, 3, 2, 4, 5).reshape(B, H, W, C)
    return np.roll(y, (SHIFT, SHIFT), axis=(1, 2))
```

```python
from contextlib import ExitStack

import numpy as np

import concourse.bass as bass
from concourse import mybir

F32 = mybir.dt.float32
F16 = mybir.dt.float16
I32 = mybir.dt.int32
ALU = mybir.AluOpType
ACT = mybir.ActivationFunctionType
AX = mybir.AxisListType.X

C = 64
WS = 7
WA = WS * WS
TOK = 2 * WA
GT = 4
GTOK = GT * TOK
HEADS, HD = 8, 8
LH, LD = 16, 4
HID = 256
NE = 8
EPS = 1e-5
SHIFT = 3
XBUF, YBUF = 4, 8
CREDIT = 12
WSCALE = 64.0


def constants():
    p = np.arange(128)
    parts = {
        "ident": np.eye(128),
        "headmask": (p[:, None] % C // HD == np.arange(HEADS)),
        "winblock": (p[:, None] // C == (np.arange(TOK) // WA)[None]),
        "winmask": (p[:, None] // WA == np.arange(2)),
        "parity": np.tile(p[:, None] // WA == np.arange(2), (1, HEADS // 2)),
        "rank": np.tile(NE - np.arange(NE), (128, 1)),
        "row": np.stack([p, p + 128], 1),
        "kvblock": (p[:, None] // LD == (np.arange(C) // LD)[None]),
        "minushalf": np.full((128, GT), -0.5),
        "eps": np.full((128, GT), EPS),
    }
    at, cols, n = {}, [], 0
    for k, v in parts.items():
        at[k] = (n, n + v.shape[1])
        cols.append(v.astype(np.float32))
        n += v.shape[1]
    return np.ascontiguousarray(np.concatenate(cols, 1)), at


def build(nc, x, cst, wqkv, bqkv, table, projw, projb, fc1w, fc1b, fc2w, fc2b, amask, rel, lnvecs, ln3,
          lwkv, lbkv, lwq, lnkvw, klnb, vlnb, lwp, lbp, wr, br, w1, b1, w2, b2, out):
    IMAGES, _, TILES, _ = x.shape
    GROUPS = TILES // GT
    NPOS = TILES * TOK
    TABLE = table.shape[0]
    _, at = constants()

    with ExitStack() as ctx:
        def sb(name, shape, dt=F32):
            return ctx.enter_context(nc.sbuf_tensor(name, shape, dt))

        def sem(name):
            return ctx.enter_context(nc.semaphore(name))

        xg = sb("xg", [TOK, XBUF, GT * C])
        yo = sb("yo", [TOK, YBUF, GT * C])
        tu_img = sb("tu_img", [TOK, TILES * C])
        ut_img = sb("ut_img", [C, TILES * TOK])
        cs = sb("cs", [128, cst.shape[1]])
        bias_ = sb("bias", [128, TILES * HEADS * WA])
        bias = bias_[0:TOK, :].rearrange("p (t c) -> p t c", t=TILES)
        wa = sb("wa", [C + 1, 3 * C])
        wq2 = sb("wq2", [C + 1, 2, C])
        wp = sb("wp", [C + 1, C])
        wf1 = sb("wf1", [C + 1, HID])
        wf2 = sb("wf2", [128, 2, C])
        wkv = sb("wkv", [C + 1, 2 * C])
        wqn = sb("wqn", [C, C + 1])
        lk = sb("lk", [C + 1, C])
        lv = sb("lv", [C + 1, C])
        wlp = sb("wlp", [C, C])
        blp = sb("blp", [C + 1, C])
        i65 = sb("i65", [C, C + 1])
        we1 = [sb(f"we1_{h}", [128, NE * HID], F16) for h in ("hi", "lo")]
        be1 = sb("be1", [128, 2 * NE])
        we2 = sb("we2", [128, NE * 2, C])
        wb2 = sb("wb2", [NE, C])
        wrt = sb("wrt", [C, NE])
        brb = sb("brb", [TOK, NE])
        fc2bias = sb("fc2bias", [TOK, C])
        m65 = sb("m65", [C + 1, C])
        st = {L: sb(f"st{L}", [TOK, GT, 6]) for L in "123ux"}
        mv = {L: sb(f"mv{L}", [TOK, GT, 2]) for L in "123ux"}
        ve = {L: sb(f"ve{L}", [TOK, GT]) for L in "123ux"}
        rs = {L: sb(f"rs{L}", [TOK, GT]) for L in "123ux"}
        z = sb("z", [TOK, GT, C])
        zt = sb("zt", [C + 1, 2 * GT, 2, WA])
        qbd = sb("qbd", [128, GT, TOK])
        kt = sb("kt", [128, GT, WA])
        kexp = sb("kexp", [128, GT, HEADS * WA])
        vexp = sb("vexp", [TOK, 2 * GT, HEADS, HD + 1])
        sc = sb("sc", [TOK, GT, HEADS * WA])
        mx = sb("mx", [TOK, GT, HEADS])
        pr = sb("pr", [TOK, GT, HEADS * WA])
        pt = sb("pt", [TOK, 2, HEADS // 2, TOK])
        rz = sb("rz", [TOK, 2, 4 * HEADS])
        rzm = sb("rzm", [TOK, 2, 4 * HEADS])
        ow = sb("ow", [TOK, 2, 4, C])
        on = sb("on", [TOK, GT, C])
        ot = sb("ot", [C + 1, GTOK])
        x1 = sb("x1", [TOK, GT, C])
        x1b = sb("x1b", [TOK, GT, C])
        z2 = sb("z2", [TOK, GT, C])
        z2t_ = sb("z2t", [C + 1, GTOK])
        hid = sb("hid", [TOK, GT, HID])
        hn = hid
        hnt = sb("hnt", [128, GT, 2, TOK])
        tt = sb("tt", [TOK, GT, C])
        u = sb("u", [TOK, GT, C])
        uts = sb("uts", [C + 1, GTOK])
        kvsq = sb("kvsq", [TOK, GT * 2 * LH, LD])
        kvss = sb("kvss", [TOK, GT * 2 * LH])
        kvsd = sb("kvsd", [TOK, GT * 2 * LH])
        kvse = sb("kvse", [TOK, GT * 2 * LH])
        kvr = sb("kvr", [TOK, GT * 2 * LH])
        kvn = sb("kvn", [TOK, 2 * GT, C + 1])
        gsum = sb("gsum", [C + 1, C + 1])
        t1s = sb("t1s", [C + 1, C])
        kvb = sb("kvb", [C, C])
        m2 = sb("m2", [C, C + 1])
        utc = sb("utc", [C + 1, GTOK])
        gp = sb("gp", [TOK, GT, C])
        t2 = sb("t2", [TOK, GT, C])
        v3 = sb("v3", [TOK, 6, GT])
        xn = sb("xn", [TOK, GT, 2, C])
        xnt = sb("xnt", [128, GTOK])
        xs = sb("xs", [128, GTOK], F16)
        lg = sb("lg", [TOK, 12, GT, NE])
        lm = sb("lm", [TOK, 8, GT])
        gate = sb("gate", [TOK, GT, NE])
        gtt = sb("gtt", [NE, GTOK])
        gate2 = sb("gate2", [TOK, 2, GT, NE])
        yacc = sb("yacc", [TOK, 2, GT * C])
        ht = sb("ht", [128, 4, GTOK])
        yg = sb("yg", [TOK, 2, GT * C])
        scratch = bias_
        relb = scratch[:, 0:WA * WA].bitcast(I32)
        hot = [scratch[:, WA * WA * h:WA * WA * (h + 1)] for h in (1, 2)]
        pos1, pos = ht[0:WA, 0, :], ht[0:TOK, 1, :]

        ps = [ctx.enter_context(nc.psum_tensor(f"ps{i}", [128, 512], F32)) for i in range(8)]
        pA, pO, pP, pS, pB, pH0, pH1, pY = ps
        pH = [pH0, pH1]

        def k(name):
            a, b = at[name]
            return cs[:, a:b]

        ident = k("ident")

        ROUTE_DIFF = 13
        COUNTS = dict(
            **{f"{s}_{L}": 1 + (s + L == "stats3") for L in "123ux" for s in ("stats", "meanvar", "vareps", "rstd")},
            z_ready=1, zT_psum=1, zT_ready=1, q_psum=1, q_ready=1, k_psum=1, kT_ready=1, v_psum=1,
            vexp_ready=1, kexp_dve=2, kexp_pool=2, score_psum=4, score_bias=4, score_max=4,
            score_sub=4, prob_ready=1, pT_psum=4, pT_ready=4, o_psum=2, o_recip=2, o_rmask=2,
            o_scaled=2, o_ready=2, oT_psum=1, oT_ready=1, proj_psum=1, x1_ready=1, x1b_ready=1, z2_ready=1,
            z2T_psum=1, z2T_ready=1, fc1_psum=2, hid_ready=2, hn_ready=1, hnT_psum=2,
            hnT_ready=2, fc2_psum=1, t_ready=1, u_ready=1, tu_ready=1, uT_psum=1, uT_ready=1,
            uT_kept=1, kv_psum=1, kv_square=1, kv_ss=1, kv_sd=1, kv_se=1, kv_r=1, kv_ready=1,
            g_psum=1, g_ready=1,
            utc_ready=1, lproj_psum=1, gelu_ready=1, t2_ready=1, x_v3=3, x_rstd3=1, x_scale=2, xn_ready=1,
            xnT_psum=1, xnT_ready=1, logit_psum=1, route=ROUTE_DIFF + 4, top_diff=1, tanh_ready=1, gate_ready=1, gate2_ready=1, gateT_psum=1,
            gateT_ready=1, gbias_psum=1, yinit_ready=1,
            xhi_ready=1, xs_ready=1, e1_psum=16, h_ready=16, e2_psum=8, yg_ready=8, y_sum=8,
        )
        S = {name: sem(name) for name in COUNTS}
        x_in, x_out, setup, setup_pos, setup_w1, setup_pe, setup_dve, mix_pe, mix_dve = (sem(n) for n in (
            "x_in", "x_out", "setup", "setup_pos", "setup_w1", "setup_pe", "setup_dve", "mix_pe", "mix_dve"))

        def credit(eng, names):
            for name in names.split():
                eng.sem_inc(S[name], COUNTS[name] * CREDIT)

        held = {e: sem(f"held_{e}") for e in ("pe", "dve", "pool", "sp")}

        def now(eng, name, n, t=0, alone=None):
            if isinstance(n, int) and n < 0:
                return
            eng.wait_ge(S[name], COUNTS[name] * (n + CREDIT) + (t + 1))
            if alone:
                eng.sem_inc(held[alone], 1)

        def before(eng, name, n, t=None):
            now(eng, name, n - 1, COUNTS[name] - 1 if t is None else t)

        def spread_keys(eng, t):
            return eng.tensor_tensor(kexp[:, t, :].rearrange("p (h k) -> p h k", k=WA),
                                     kt[:, t, :].unsqueeze(1).to_broadcast([128, HEADS, WA]),
                                     k("headmask").unsqueeze(2).to_broadcast([128, HEADS, WA]), ALU.mult)

        def cols(t):
            return slice(TOK * t, TOK * (t + 1))

        SETUP_LOADS = []

        def load(dst, src):
            SETUP_LOADS.append((dst, src))

        row = slice(C, C + 1)
        w1raw = scratch[:, 3 * WA * WA:3 * WA * WA + NE * HID]
        w1tmp = scratch[:, 3 * WA * WA + NE * HID:3 * WA * WA + 2 * NE * HID]
        load(cs[:, :], cst)
        load(wa[0:C, :], wqkv)
        load(wa[row, :], bqkv)
        load(wp[0:C, :], projw)
        load(wp[row, :], projb)
        load(wf1[0:C, :], fc1w)
        load(wf1[row, :], fc1b)
        load(wf2[:, :, :], fc2w)
        load(wkv[0:C, :], lwkv)
        load(wkv[row, :], lbkv)
        load(wqn[:, :], lwq)
        load(lk[row, :], klnb)
        load(lv[row, :], vlnb)
        load(wlp[:, :], lwp)
        load(blp[row, :], lbp)
        for half in range(2):
            load(w1raw[C * half:C * (half + 1), :], w1)
        load(be1[:, :], b1)
        load(we2[:, :, :], w2)
        load(wb2[:, :], b2)
        load(wrt[:, :], wr)
        load(brb[:, :], br.partition_broadcast(TOK))
        vecs = sb("vecs", [C, 4 + 2 * NE])
        vec3 = sb("vec3", [128, 4])
        kvw = sb("kvw", [C, 2])
        f2row = sb("f2row", [1, C])
        load(vecs[:, :], lnvecs)
        lng2 = sb("lng2", [128, NE])
        for half in range(2):
            load(lng2[C * half:C * (half + 1), :], lnvecs[:, 4:4 + NE])
        load(vec3[:, :], ln3)
        load(kvw[:, :], lnkvw)
        load(f2row[:, :], fc2b)
        load(relb, rel.partition_broadcast(128))
        mask_sb = tu_img[:, 0:TILES * WA]
        for w in range(2):
            load(mask_sb[w * WA:(w + 1) * WA, :].rearrange("q (p k) -> q p k", k=WA),
                 amask.rearrange("(p w) q k -> w q p k", w=2)[w])
        tab = sb("tab", [128, 2, HEADS])
        load(tab[:, 0, :], table[0:128, :])
        load(tab[0:TABLE - 128, 1, :], table[128:TABLE, :])
        ln3bb = sb("ln3bb", [128, 2, TOK])
        ones = sb("ones", [128, TOK])

        block = ctx.enter_context(nc.Block())

        ORDER = dict(
            pe="""lp:-9 in0:-10 q:+1 mix0:+0 in1:-10 in2:-10 out7:-11 mix1:+0 s0:+1 in3:-10 out0:-10 in4:-10 mix2:+0 s1:+1
                  in5:-10 z2T:+0 in6:-10 s2:+1 fc10:+0 fc11:+0 s3:+1 out1:-10 in7:-10 xnT:-9 v:+1 logit:-9 out2:-10
                  in8:-10 in9:-10 pT0:+1 out3:-10 hT0:+0 hT1:+0 in10:-10 pT1:+1 fc2:+0 o0:+1 o1:+1 mix3:+0 pT2:+1 out4:-10
                  pT3:+1 in11:-10 o2:+1 gT:-9 o3:+1 uT:+0 gb:-9 in12:-10 in13:-10 kv:+0 oT:+1 out5:-10 proj:+1 in14:-10
                  in15:-10 zT:+2 out6:-10 k:+2 G:+0 mix4:+0""",
            dve="""mv2:+0 g6:-11 ke0:+1 qbd:+1 t2:-9 mix0:+0 stx:-9 mix1:+0 g7:-11 mvx:-9 ke2:+1 sb0:+1 z2:+0 g0:-10 sb1:+1
                   mx0:+1 mix2:+0 st1:+2 sb2:+1 mx1:+1 mx2:+1 xn:-9 sb3:+1 mx3:+1 st30:+0 st31:+0 g1:-10 mv3:+0 rt0:-9
                   ve:+1 rt1:-9 rt2:-9 g2:-10 rt3:-9 hn:+0 rt4:-9 rt5:-9 mv1:+2 rt6:-9 rt7:-9 utc:-8 rt8:-9 rt9:-9 g3:-10
                   rt10:-9 rt11:-9 t:+0 rt12:-9 stu:+0 rt13:-9 mvu:+0 rc0:+1 tw:-9 rm0:+1 ow0:+1 w:-9 mix3:+0 gate:-9 u:+0
                   g4:-10 on0:+1 rc1:+1 rm1:+1 yinit:-9 ow1:+1 on1:+1 z:+2 kvss:+0 g5:-10 x1:+1 hi:-9 kve:+0 kvr:+0 kvn:+0
                   lo:-9 st2:+1 Gsum:+0""",
            act="""lpg:-9 h0:-10 h1:-10 h2:-10 h3:-10 h4:-10 z2t:+0 ge0:+0 ge1:+0 h5:-10 h6:-10 h7:-10 xnt:-9 exp:+1 h8:-10
                   pt0:+1 hnt0:+0 hnt1:+0 h9:-10 h10:-10 pt1:+1 tanh:-9 pt2:+1 pt3:+1 gtt:-9 h11:-10 utk:+0 uts:+0 h12:-10
                   h13:-10 sq:+0 ot:+1 sd:+0 zt:+2 h14:-10 h15:-10 kt:+2""",
            pool="""x1b:+0 ke1:+1 y5:-11 r2:+0 y6:-11 ke3:+1 pw2:+0 rx:-9 pwx:-9 v0:-9 v1:-9 v2:-9 v3:-9 v4:-9 sub0:+1
                    y7:-11 sub1:+1 sub2:+1 sub3:+1 tu:-1 y0:-10 r3:+0 pw3:+0 y1:-10 y2:-10 r1:+2 ru:+0 pwu:+0 y3:-10 pw1:+2
                    y4:-10""",
        )
        ran = {}
        PLAN = {eng: [(step.split(":")[0], int(step.split(":")[1])) for step in order.split()] for eng, order in ORDER.items()}

        def images(eng, plan, steps):
            total = IMAGES * GROUPS

            def active(n):
                return [n % GROUPS == 0 and 0 < n <= total if name[:3] == "mix" else n + at in range(total)
                        for name, at in plan]

            def iteration(i, j, runs):
                n = i * GROUPS + j
                ran.clear()
                ran.update({name: at for (name, at), run in zip(plan, runs) if run})
                ran["image"] = i - 1
                for (name, at), run in zip(plan, runs):
                    if run and name[:3] == "mix":
                        steps[name](i - 1, 0)
                    elif run:
                        steps[name](n + at, (j + at + 2 * GROUPS) % GROUPS)

            def image(i, like=None):
                runs = [active((i if like is None else like) * GROUPS + j) for j in range(GROUPS)]
                first = 0
                while first < GROUPS:
                    stop = first + 1
                    while stop < GROUPS and runs[stop] == runs[first]:
                        stop += 1
                    if stop > first + 1:
                        with eng.Fori(first, stop) as j:
                            iteration(i, j, runs[first])
                    elif any(runs[first]):
                        iteration(i, first, runs[first])
                    first = stop

            image(-1)
            image(0)
            image(1)
            if IMAGES > 3:
                with eng.Fori(2, IMAGES - 1) as i:
                    image(i, 2)
            image(IMAGES - 1)
            image(IMAGES)
            image(IMAGES + 1)

        @block.sync
        def _(sp):
            sp.sem_inc(x_out, 16 * YBUF)
            for dst, src in SETUP_LOADS:
                sp.dma_start(dst, src).then_inc(setup, 16)

            def load_x(n, i, j):
                if not (isinstance(n, int) and n == 0):
                    sp.wait_ge(x_in, 16 * n)
                    sp.sem_inc(held["sp"], 1)
                now(sp, "x1_ready", n - XBUF, alone="sp")
                sp.dma_start(xg[:, bass.ts(n % XBUF, 1), :],
                             x[bass.ts(i, 1), :, bass.ts(j, GT), :].rearrange("o p t c -> p o (t c)")).then_inc(x_in, 16)

            def store_y(n, i, j):
                now(sp, "y_sum", n, NE - 1, alone="sp")
                sp.wait_ge(x_out, 16 * (n + YBUF))
                sp.sem_inc(held["sp"], 1)
                sp.dma_start(out[bass.ts(i, 1), :, bass.ts(j, GT), :].rearrange("o p t c -> p o (t c)"),
                             yo[:, bass.ts(n % YBUF, 1), :]).then_inc(x_out, 16)

            for j in range(XBUF):
                load_x(j, 0, j)
            sp.wait_ge(setup_dve, 8)
            for w in range(2):
                sp.dma_start(pos[w * WA:(w + 1) * WA, :], pos1).then_inc(setup_pos, 16)
            with sp.Fori(XBUF, GROUPS) as j:
                load_x(j, 0, j)
            with sp.Fori(1, 2) as i:
                with sp.Fori(0, GROUPS) as j:
                    load_x(i * GROUPS + j, i, j)
            with sp.Fori(2, IMAGES) as i:
                with sp.Fori(0, GROUPS) as j:
                    load_x(i * GROUPS + j, i, j)
                    store_y(i * GROUPS + j - 2 * GROUPS, i - 2, j)
            with sp.Fori(IMAGES - 2, IMAGES) as i:
                with sp.Fori(0, GROUPS) as j:
                    store_y(i * GROUPS + j, i, j)
            sp.wait_ge(x_out, 16 * (IMAGES * GROUPS + YBUF))

        @block.tensor
        def _(pe):
            pe.wait_ge(setup, 16 * len(SETUP_LOADS))
            pe.wait_ge(setup_dve, 2)
            pe.matmul(pB[C:C + 1, 0:3 * C], vecs[:, 1:2], wa[0:C, :], start=True, stop=True)
            pe.matmul(pP[C:C + 1, 0:HID], vecs[:, 3:4], wf1[0:C, :], start=True, stop=True).then_inc(setup_pe, 1)
            for b in range(2 * NE):
                pe.matmul(pH0[:, b:b + 1], w1raw[0:C, 128 * b:128 * (b + 1)], vecs[:, 4 + NE + b // 2:5 + NE + b // 2],
                          start=True, stop=True)
            for h in range(2):
                pe.matmul(pA[0:TOK, 0:C], ln3bb[:, h, :], wf2[:, h, :], start=(h == 0), stop=False)
            pe.matmul(pA[0:TOK, 0:C], ones[0:1, :], f2row[:, :], start=False, stop=True).then_inc(setup_pe, 1)
            pe.wait_ge(setup_dve, 4)
            for key in range(WA):
                for half, rows in ((0, 128), (1, TABLE - 128)):
                    at_key = hot[half][0:rows, key:WA * WA:WA]
                    last = pe.matmul(pS[0:WA, key * HEADS:(key + 1) * HEADS], at_key, tab[0:rows, half, :],
                                     start=(half == 0), stop=(half == 1))
            last.then_inc(setup_pe, 1)
            pe.wait_ge(setup_dve, 10)
            credit(pe, "zT_psum q_psum k_psum v_psum score_psum pT_psum o_psum oT_psum proj_psum z2T_psum fc1_psum "
                       "hnT_psum fc2_psum uT_psum kv_psum g_psum lproj_psum xnT_psum logit_psum gateT_psum gbias_psum "
                       "e1_psum e2_psum")

            def transposes(dst, src, signal, width=C):
                for t in range(GT):
                    last = pe.transpose(dst[0:width, cols(t)], src(t), ident[0:TOK, 0:TOK])
                last.then_inc(S[signal], 1)


            def ln1n(a, j):
                if "proj" in ran:
                    now(pe, "x1_ready", a - 1)
                elif "uT" in ran:
                    now(pe, "uT_kept", a - 2)
                else:
                    now(pe, "zT_ready", a - 1)
                now(pe, "z_ready", a, alone="pe")
                transposes(pA, lambda t: z[:, t, :], "zT_psum")

            def q(a, j):
                if "G" in ran:
                    now(pe, "g_ready", a - 2)
                elif "zT" in ran:
                    now(pe, "zT_ready", a)
                else:
                    now(pe, "x1_ready", a - 1)
                now(pe, "zT_ready", a)
                pe.matmul(pA[:, 0:GTOK], wq2[:, :, :].rearrange("p a b -> p (a b)"), zt[:, :, 0, :],
                          start=True, stop=True).then_inc(S["q_psum"], 1)

            def keys(a, j):
                now(pe, "zT_ready", a)
                before(pe, "o_scaled", a)
                for w in range(2):
                    last = pe.matmul(pO[C * w:C * (w + 1), 0:GT * WA], wa[:, C:2 * C], zt[:, w:2 * GT:2, 0, :],
                                     start=True, stop=True)
                last.then_inc(S["k_psum"], 1)

            def values(a, j):
                now(pe, "zT_ready", a)
                before(pe, "pT_ready", a)
                for t in range(2 * GT):
                    last = pe.matmul(pP[0:TOK, t * C:(t + 1) * C], zt[:, t].rearrange("p a k -> p (a k)"),
                                     wa[:, 2 * C:3 * C], start=True, stop=True)
                last.then_inc(S["v_psum"], 1)

            def score(a, t):
                now(pe, "q_ready", a)
                now(pe, "kexp_pool" if t % 2 else "kexp_dve", a, t // 2)
                now(pe, "score_bias", a - (t == 0), (t - 1) % GT)
                pe.matmul(pS[0:TOK, 0:HEADS * WA], qbd[:, t, :], kexp[:, t, :], start=True, stop=True)\
                    .then_inc(S["score_psum"], 1)

            def prob_T(a, t):
                now(pe, "prob_ready", a)
                if t == 0:
                    now(pe, "vexp_ready", a)
                else:
                    now(pe, "pT_ready", a, t - 1)
                for h in range(HEADS // 2):
                    last = pe.transpose(pP[0:TOK, cols(h)], pr[:, t, TOK * h:TOK * (h + 1)], ident[0:TOK, 0:TOK])
                last.then_inc(S["pT_psum"], 1)

            def attend(a, t):
                if t == 0:
                    now(pe, "kT_ready", a)
                    now(pe, "vexp_ready", a)
                elif t == 2:
                    now(pe, "o_scaled", a, 0)
                now(pe, "pT_ready", a, t)
                o = pO[0:TOK, (t % 2) * 144:(t % 2 + 1) * 144].rearrange("p (w h d) -> p w h d", w=2, h=HEADS)
                for h in range(HEADS // 2):
                    last = pe.matmul(o[:, :, 2 * h:2 * h + 2, :], pt[:, t % 2, h, :],
                                     vexp[:, 2 * t:2 * t + 2, 2 * h:2 * h + 2, :], start=True, stop=True)
                if t % 2:
                    last.then_inc(S["o_psum"], 1)

            def oT(a, j):
                if "uT" in ran:
                    now(pe, "uT_kept", a - 1)
                else:
                    now(pe, "q_ready", a)
                now(pe, "o_ready", a, 1, alone="pe")
                transposes(pA, lambda t: on[:, t, :], "oT_psum")

            def proj(a, j):
                now(pe, "oT_ready", a)
                for t in range(GT):
                    last = pe.matmul(pA[0:TOK, C * t:C * (t + 1)], ot[:, cols(t)], wp[:, :], start=True, stop=True)
                last.then_inc(S["proj_psum"], 1)

            def z2t(n, j):
                if "q" in ran:
                    now(pe, "q_ready", n + 1)
                else:
                    now(pe, "g_ready", n - 1)
                now(pe, "z2_ready", n, alone="pe")
                transposes(pA, lambda t: z2[:, t, :], "z2T_psum")

            def fc1(n, half):
                if half == 0:
                    if "mix2" in ran:
                        pe.wait_ge(mix_dve, 5 * ran["image"] + 4)
                    elif "lp" in ran:
                        now(pe, "gelu_ready", n - GROUPS - 1)
                    else:
                        now(pe, "kv_ready", n - 1)
                else:
                    now(pe, "z2T_ready", n)
                now(pe, "z2T_ready", n)
                for t in (2 * half, 2 * half + 1):
                    last = pe.matmul((pB, pA)[half][0:TOK, (t % 2) * HID:(t % 2 + 1) * HID], z2t_[:, cols(t)], wf1[:, :],
                                     start=True, stop=True)
                last.then_inc(S["fc1_psum"], 1)

            def hidden_T(n, half):
                if half == 0:
                    if "logit" in ran:
                        now(pe, "route", n - GROUPS - 1)
                    else:
                        now(pe, "hid_ready", n)
                else:
                    now(pe, "hid_ready", n, 1)
                now(pe, "hn_ready", n)
                for t in (2 * half, 2 * half + 1):
                    for h in range(2):
                        last = pe.transpose((pB, pA)[half][:, TOK * (2 * (t % 2) + h):TOK * (2 * (t % 2) + h + 1)],
                                            hn[:, t, 128 * h:128 * (h + 1)], ident[0:TOK, 0:TOK])
                last.then_inc(S["hnT_psum"], 1)

            def fc2(n, j):
                now(pe, "hnT_ready", n)
                for t in range(GT):
                    if t % 2 == 0:
                        now(pe, "hnT_ready", n, t // 2)
                    for h in range(2):
                        last = pe.matmul(pB[0:TOK, C * t:C * (t + 1)], hnt[:, t, h, :], wf2[:, h, :],
                                         start=(h == 0), stop=(h == 1))
                last.then_inc(S["fc2_psum"], 1)

            def ut(n, j):
                now(pe, "hnT_ready", n, 1)
                now(pe, "u_ready", n, alone="pe")
                transposes(pA, lambda t: u[:, t, :], "uT_psum")

            def kv(n, j):
                if "gb" in ran:
                    now(pe, "yinit_ready", n - GROUPS - 1)
                elif "mix3" in ran:
                    pe.wait_ge(mix_dve, 5 * ran["image"] + 5)
                else:
                    now(pe, "t_ready", n)
                now(pe, "uT_ready", n)
                for t in range(GT):
                    last = pe.matmul(pB[0:TOK, 128 * t:128 * (t + 1)], uts[:, cols(t)], wkv[:, :], start=True, stop=True)
                last.then_inc(S["kv_psum"], 1)

            def kvsum(n, j):
                if "zT" in ran:
                    now(pe, "zT_ready", n + 2)
                elif "proj" in ran:
                    now(pe, "x1_ready", n + 1)
                else:
                    now(pe, "uT_kept", n)
                now(pe, "kv_ready", n)
                for t in range(GT):
                    last = pe.matmul(pA[0:C + 1, 0:C + 1], kvn[:, 2 * t, :], kvn[:, 2 * t + 1, :],
                                     start=(t == 0), stop=(t == GT - 1))
                last.then_inc(S["g_psum"], 1)

            def mix(i, part):
                n = (i + 1) * GROUPS
                if part == 0:
                    if "lp" in ran:
                        now(pe, "gelu_ready", n - GROUPS - 1)
                    elif "kv" in ran:
                        now(pe, "kv_ready", n - 1)
                elif part == 3:
                    if "fc2" in ran:
                        now(pe, "t_ready", n)
                    elif "logit" in ran:
                        now(pe, "route", n - GROUPS - 1)
                out_ = pB[:, 0:C + 1]
                if part == 4:
                    pe.wait_ge(mix_dve, 5 * i + 5)
                    pe.sem_inc(held["pe"], 1)
                    return
                if part == 0:
                    now(pe, "g_ready", (i + 1) * GROUPS - 1)
                    last = pe.matmul(out_[0:C + 1, 0:C], gsum[:, :], lk[:, :], start=True, stop=True)
                elif part == 1:
                    pe.wait_ge(mix_dve, 5 * i + 1)
                    last = pe.matmul(out_[0:C, 0:C], t1s[:, :], lv[:, :], start=True, stop=True)
                elif part == 2:
                    pe.wait_ge(mix_dve, 5 * i + 3)
                    pe.sem_inc(held["pe"], 1)
                    last = pe.matmul(out_[0:C, 0:C + 1], kvb[:, :], wqn[:, :], start=True, stop=True)
                else:
                    pe.wait_ge(mix_dve, 5 * i + 4)
                    last = pe.matmul(out_[0:C + 1, 0:C], m2[:, :], wlp[:, :], start=True, stop=True)
                last.then_inc(mix_pe, 1)

            def gp_(c, j):
                if "kv" in ran:
                    now(pe, "kv_ready", c + GROUPS)
                else:
                    now(pe, "yinit_ready", c - 1)
                now(pe, "utc_ready", c)
                for t in range(GT):
                    last = pe.matmul(pB[0:TOK, C * t:C * (t + 1)], utc[:, cols(t)], m65[:, :], start=True, stop=True)
                last.then_inc(S["lproj_psum"], 1)

            def gpn(c, j):
                if "fc10" in ran:
                    now(pe, "hid_ready", c + GROUPS + 1)
                elif "mix2" in ran:
                    pe.wait_ge(mix_dve, 5 * ran["image"] + 4)
                else:
                    now(pe, "gelu_ready", c)
                now(pe, "xn_ready", c)
                transposes(pB, lambda t: xn[:, t, :, :].rearrange("p a c -> p (a c)"), "xnT_psum", 2 * C)

            def logits(c, j):
                now(pe, "xnT_ready", c)
                now(pe, "xnT_ready", c)
                pe.sem_inc(held["pe"], 1)
                for t in range(GT):
                    last = pe.matmul(pB[0:TOK, NE * t:NE * (t + 1)], xnt[0:C, cols(t)], wrt[:, :], start=True, stop=True)
                last.then_inc(S["logit_psum"], 1)

            def gates(c, j):
                if "mix3" in ran:
                    pe.wait_ge(mix_dve, 5 * ran["image"] + 5)
                elif "fc2" in ran:
                    now(pe, "t_ready", c + GROUPS + 1)
                else:
                    now(pe, "route", c)
                now(pe, "gate_ready", c, alone="pe")
                transposes(pB, lambda t: gate[:, t, :], "gateT_psum", NE)

            def gbias(c, j):
                now(pe, "gateT_ready", c)
                now(pe, "gateT_ready", c)
                pe.sem_inc(held["pe"], 1)
                for t in range(GT):
                    last = pe.matmul(pB[0:TOK, C * t:C * (t + 1)], gtt[:, cols(t)], wb2[:, :], start=True, stop=True)
                last.then_inc(S["gbias_psum"], 1)

            def expert_in(d, b):
                if b == 0:
                    now(pe, "xs_ready", d)
                now(pe, "h_ready", d - (b < 2), (b - 2) % (2 * NE))
                for half in range(2):
                    last = pe.matmul(pH[b % 2][:, 0:GTOK], we1[half][:, 128 * b:128 * (b + 1)], xs[:, :],
                                     start=(half == 0), stop=(half == 1))
                last.then_inc(S["e1_psum"], 1)

            def expert_out(d, e):
                now(pe, "h_ready", d, 2 * e + 1)
                now(pe, "yg_ready", d - (e == 0), (e - 1) % NE)
                for t in range(GT):
                    for h in range(2):
                        last = pe.matmul(pY[0:TOK, C * t:C * (t + 1)], ht[:, 2 * (e % 2) + h, cols(t)], we2[:, 2 * e + h, :],
                                         start=(h == 0), stop=(h == 1))
                last.then_inc(S["e2_psum"], 1)

            steps = dict(zT=ln1n, q=q, k=keys, v=values, oT=oT, proj=proj, z2T=z2t, fc2=fc2, uT=ut, kv=kv, G=kvsum,
                         lp=gp_, xnT=gpn, logit=logits, gT=gates, gb=gbias)
            for t in range(GT):
                steps[f"s{t}"] = lambda a, j, t=t: score(a, t)
                steps[f"pT{t}"] = lambda a, j, t=t: prob_T(a, t)
                steps[f"o{t}"] = lambda a, j, t=t: attend(a, t)
            for half in range(2):
                steps[f"fc1{half}"] = lambda n, j, half=half: fc1(n, half)
                steps[f"hT{half}"] = lambda n, j, half=half: hidden_T(n, half)
            for b in range(2 * NE):
                steps[f"in{b}"] = lambda d, j, b=b: expert_in(d, b)
            for e in range(NE):
                steps[f"out{e}"] = lambda d, j, e=e: expert_out(d, e)
            for part in range(5):
                steps[f"mix{part}"] = lambda i, j, part=part: mix(i, part)
            images(pe, PLAN["pe"], steps)

        @block.vector
        def _(ve_):
            dve = ve_
            dve.wait_ge(setup, 16 * len(SETUP_LOADS))
            dve.memset(ones[:, :], 1.0).then_inc(setup_dve, 1)
            dve.wait_ge(setup_dve, 1)
            for h in range(2):
                last = dve.tensor_scalar(ln3bb[:, h, :], ones[:, :], vec3[:, 2 + h:3 + h], None, ALU.mult)
            last.then_inc(setup_dve, 1)
            for h, rows in ((0, 128), (1, TABLE - 128)):
                last = dve.tensor_scalar(hot[h][0:rows, :], relb[0:rows, :], k("row")[0:rows, h:h + 1], None, ALU.is_equal)
            last.then_inc(setup_dve, 2)
            dve.memset(blp[0:C, :], 0.0)
            dve.memset(i65[:, C:C + 1], 0.0)
            dve.tensor_copy(i65[:, 0:C], ident[0:C, 0:C])
            for ones_row in (zt[row], ot[row, :], z2t_[row, :], uts[row, :], utc[row, :]):
                dve.memset(ones_row, 1.0)
            dve.memset(kvn[:, :, C:C + 1], 1.0)
            dve.tensor_copy(vexp[:, :, :, HD], k("parity")[0:TOK].unsqueeze(1).to_broadcast([TOK, 2 * GT, HEADS]))
            dve.memset(gsum[:, :], 0.0)
            dve.tensor_scalar(lk[0:C, :], ident[0:C, 0:C], kvw[:, 0:1], None, ALU.mult)
            dve.tensor_scalar(lv[0:C, :], ident[0:C, 0:C], kvw[:, 1:2], None, ALU.mult)
            dve.tensor_reduce(kvss[0:C + 1, 0:2 * LH], wkv[:, :].rearrange("p (g d) -> p g d", d=LD), AX, ALU.add)\
                .then_inc(setup_dve, 1)
            dve.wait_ge(setup_dve, 5)
            dve.scalar_tensor_tensor(out=wkv[:, :].rearrange("p (g d) -> p g d", d=LD),
                                     in0=kvss[0:C + 1, 0:2 * LH].unsqueeze(2).to_broadcast([C + 1, 2 * LH, LD]),
                                     scalar=-1.0 / LD, in1=wkv[:, :].rearrange("p (g d) -> p g d", d=LD),
                                     op0=ALU.mult, op1=ALU.add)
            dve.wait_ge(setup_pe, 2)
            dve.tensor_tensor(wa[row, :], pB[row, 0:3 * C], wa[row, :], ALU.add)
            dve.tensor_scalar(wa[0:C, :], wa[0:C, :], vecs[:, 0:1], None, ALU.mult)
            dve.tensor_tensor(wf1[row, :], pP[row, 0:HID], wf1[row, :], ALU.add)
            dve.tensor_scalar(wf1[0:C, :], wf1[0:C, :], vecs[:, 2:3], None, ALU.mult)
            dve.tensor_tensor(be1[:, :], pH0[:, 0:2 * NE], be1[:, :], ALU.add)
            for e in range(NE):
                part = slice(e * HID, (e + 1) * HID)
                last = dve.tensor_scalar(w1tmp[:, part], w1raw[:, part], lng2[:, e:e + 1], WSCALE, ALU.mult, ALU.mult)
            last.then_inc(setup_w1, 1)
            dve.wait_ge(setup_w1, 1)
            dve.tensor_copy(we1[0][:, :], w1tmp).then_inc(setup_w1, 1)
            dve.wait_ge(setup_w1, 2)
            dve.tensor_tensor(we1[1][:, :], w1tmp, we1[0][:, :], ALU.subtract).then_inc(setup_w1, 1)
            dve.wait_ge(setup_w1, 3)
            for h in range(2):
                dve.tensor_scalar(wf2[:, h, :], wf2[:, h, :], vec3[:, h:h + 1], None, ALU.mult)
            dve.tensor_copy(fc2bias[:, :], pA[0:TOK, 0:C]).then_inc(setup_dve, 1)
            dve.wait_ge(setup_dve, 6)
            for w in range(2):
                dve.tensor_scalar(wq2[:, w, :], wa[:, 0:C], float(HD) ** -0.5, None, ALU.mult)
            dve.wait_ge(setup_pe, 3)
            dve.tensor_copy(pos1.rearrange("p (h k) -> p h k", k=WA),
                            pS[0:WA, 0:WA * HEADS].rearrange("p (k h) -> p h k", h=HEADS)).then_inc(setup_dve, 2)
            dve.wait_ge(setup_pos, 32)
            for t in range(TILES):
                last = dve.tensor_tensor(bias[:, t, :].rearrange("p (h k) -> p h k", k=WA),
                                         pos.rearrange("p (h k) -> p h k", k=WA),
                                         mask_sb[:, t * WA:(t + 1) * WA].unsqueeze(1).to_broadcast([TOK, HEADS, WA]), ALU.add)
            last.then_inc(setup_dve, 2)
            dve.wait_ge(setup_dve, 10)
            credit(dve, "stats_1 stats_2 stats_3 stats_u stats_x meanvar_1 meanvar_2 meanvar_3 meanvar_u meanvar_x z_ready "
                        "q_ready vexp_ready kexp_dve score_bias score_max o_recip o_rmask o_scaled o_ready "
                        "x1_ready z2_ready hn_ready t_ready u_ready kv_ss kv_se kv_r kv_ready g_ready utc_ready t2_ready "
                        "xn_ready route top_diff gate_ready gate2_ready yg_ready yinit_ready xhi_ready xs_ready")

            def statistics(n, L, tiles):
                for t in range(GT):
                    last = dve.bn_stats(st[L][:, t, :], tiles(t))
                last.then_inc(S[f"stats_{L}"], 1)

            def mean_variance(n, L):
                now(dve, f"stats_{L}", n, COUNTS[f"stats_{L}"] - 1, alone="dve")
                for t in range(GT):
                    last = dve.bn_aggr(mv[L][:, t, :], st[L][:, t, :])
                last.then_inc(S[f"meanvar_{L}"], 1)

            def normalize(n, L, dst, tiles, signal):
                now(dve, f"rstd_{L}", n)
                for t in range(GT):
                    last = dve.tensor_scalar(dst[:, t, :], tiles(t), mv[L][:, t, 0:1], rs[L][:, t:t + 1],
                                             ALU.subtract, ALU.mult)
                last.then_inc(S[signal], 1)

            def x_tile(n, t):
                return xg[:, bass.ts(n % XBUF, 1), C * t:C * (t + 1)].rearrange("p a c -> p (a c)")

            def ln1(a, j):
                dve.wait_ge(x_in, 16 * (a + 1))
                statistics(a, "1", lambda t: x_tile(a, t))

            def ln1n(a, j):
                before(dve, "zT_psum", a)
                normalize(a, "1", z, lambda t: x_tile(a, t), "z_ready")

            def q_blocks(a, j):
                now(dve, "q_psum", a)
                before(dve, "score_psum", a)
                dve.tensor_tensor(qbd[:, :, :], pA[:, 0:GTOK].rearrange("p (t c) -> p t c", c=TOK),
                                  k("winblock").unsqueeze(1).to_broadcast([128, GT, TOK]), ALU.mult)\
                    .then_inc(S["q_ready"], 1)

            def expand_keys(a, t):
                now(dve, "kT_ready", a)
                before(dve, "score_psum", a)
                spread_keys(dve, t).then_inc(S["kexp_dve"], 1)

            def expand_values(a, j):
                now(dve, "v_psum", a)
                before(dve, "o_psum", a)
                dve.tensor_tensor(vexp[:, :, :, 0:HD], pP[0:TOK, :].rearrange("p (t h d) -> p t h d", h=HEADS, d=HD),
                                  k("parity")[0:TOK].unsqueeze(1).unsqueeze(3).to_broadcast([TOK, 2 * GT, HEADS, HD]),
                                  ALU.mult).then_inc(S["vexp_ready"], 1)

            def add_bias(a, j, t):
                now(dve, "score_psum", a, t)
                before(dve, "prob_ready", a)
                dve.tensor_tensor(sc[:, t, :], pS[0:TOK, 0:HEADS * WA],
                                  bias[:, bass.ds(j * GT + t, 1), :].rearrange("p a b -> p (a b)"), ALU.add)\
                    .then_inc(S["score_bias"], 1)

            def largest(a, t):
                now(dve, "score_bias", a, t)
                dve.tensor_reduce(mx[:, t, :], sc[:, t, :].rearrange("p (h k) -> p h k", k=WA), AX, ALU.max)\
                    .then_inc(S["score_max"], 1)

            def heads_out(n, half):
                now(dve, "o_psum", n, half)
                o = pO[0:TOK, 0:288].rearrange("p (t h d) -> p t h d", t=4, d=HD + 1)
                dve.reciprocal(rz[:, half, :].rearrange("p (t h) -> p t h", h=HEADS), o[:, :, :, HD]).then_inc(S["o_recip"], 1)

            def own_window(n, half):
                now(dve, "o_recip", n, half)
                dve.tensor_tensor(rzm[:, half, :].rearrange("p (t w h) -> p t w h", t=2, w=2),
                                  rz[:, half, :].rearrange("p (t w h) -> p t w h", t=2, w=2),
                                  k("winmask")[0:TOK].unsqueeze(1).unsqueeze(3).to_broadcast([TOK, 2, 2, HEADS]),
                                  ALU.mult).then_inc(S["o_rmask"], 1)

            def scale_heads(n, half):
                o = pO[0:TOK, 0:288].rearrange("p (t h d) -> p t h d", t=4, d=HD + 1)
                now(dve, "o_rmask", n, half)
                dve.tensor_tensor(ow[:, half].rearrange("p t (h d) -> p t h d", d=HD), o[:, :, :, 0:HD],
                                  rzm[:, half, :].rearrange("p (t h) -> p t h", h=HEADS).unsqueeze(3)
                                  .to_broadcast([TOK, 4, HEADS, HD]), ALU.mult).then_inc(S["o_scaled"], 1)

            def join_windows(n, half):
                now(dve, "o_scaled", n, half)
                if half == 0:
                    before(dve, "oT_psum", n)
                pair = ow[:, half].rearrange("p (t w) c -> p t w c", w=2)
                dve.tensor_tensor(on[:, 2 * half:2 * half + 2, :], pair[:, :, 0], pair[:, :, 1], ALU.add)\
                    .then_inc(S["o_ready"], 1)

            def proj(a, j):
                now(dve, "proj_psum", a)
                before(dve, "x1b_ready", a)
                dve.tensor_tensor(x1[:, :, :], pA[0:TOK, 0:GT * C].rearrange("p (t c) -> p t c", c=C),
                                  xg[:, bass.ts(a % XBUF, 1), :].rearrange("p a (t c) -> p (a t) c", c=C), ALU.add)\
                    .then_inc(S["x1_ready"], 1)

            def stats2(a, j):
                now(dve, "x1_ready", a)
                statistics(a, "2", lambda t: x1[:, t, :])

            def z2n(a, j):
                before(dve, "z2T_psum", a)
                normalize(a, "2", z2, lambda t: x1[:, t, :], "z2_ready")

            def stats3(n, half):
                now(dve, "hid_ready", n, half)
                for t in (2 * half, 2 * half + 1):
                    last = dve.bn_stats(st["3"][:, t, :], hid[:, t, :])
                last.then_inc(S["stats_3"], 1)

            def ln3n(n, j):
                normalize(n, "3", hn, lambda t: hid[:, t, :], "hn_ready")

            def fc2(n, j):
                now(dve, "fc2_psum", n)
                now(dve, "x1b_ready", n)
                before(dve, "tu_ready", n)
                dve.tensor_tensor(tt[:, :, :], pB[0:TOK, 0:GT * C].rearrange("p (t c) -> p t c", c=C),
                                  x1b[:, :, :], ALU.add).then_inc(S["t_ready"], 1)

            def statsu(n, j):
                now(dve, "t_ready", n)
                statistics(n, "u", lambda t: tt[:, t, :])

            def ut(n, j):
                before(dve, "uT_psum", n)
                normalize(n, "u", u, lambda t: tt[:, t, :], "u_ready")

            def kv(n, j):
                now(dve, "kv_square", n)
                dve.tensor_reduce(kvss[:, :], kvsq[:, :, :], AX, ALU.add).then_inc(S["kv_ss"], 1)

            def kvsum(n, j):
                now(dve, "kv_sd", n)
                dve.tensor_scalar(kvse[:, :], kvsd[:, :], EPS, None, ALU.add).then_inc(S["kv_se"], 1)

            def deviation_recip(n, j):
                now(dve, "kv_se", n)
                dve.reciprocal(kvr[:, :], kvse[:, :]).then_inc(S["kv_r"], 1)

            def scale_kv(n, j):
                now(dve, "kv_r", n)
                before(dve, "g_psum", n)
                dve.tensor_tensor(kvn[:, :, 0:C].rearrange("p t (h d) -> p t h d", d=LD),
                                  pB[0:TOK, :].rearrange("p (t h d) -> p t h d", h=LH, d=LD),
                                  kvr[:, :].rearrange("p (t h) -> p t h", h=LH).unsqueeze(3)
                                  .to_broadcast([TOK, 2 * GT, LH, LD]), ALU.mult).then_inc(S["kv_ready"], 1)

            def add_G(n, j):
                now(dve, "g_psum", n)
                before(dve, "g_ready", n)
                if "mix3" in ran:
                    dve.wait_ge(mix_dve, 5 * ran["image"] + 2)
                dve.tensor_tensor(gsum[:, :], pA[0:C + 1, 0:C + 1], gsum[:, :], ALU.add).then_inc(S["g_ready"], 1)

            def mix(i, part):
                out_ = pB[:, 0:C + 1]
                dve.wait_ge(mix_pe, 4 * i + part + 1)
                if part == 0:
                    dve.tensor_copy(t1s[:, :], out_[0:C + 1, 0:C]).then_inc(mix_dve, 1)
                    dve.memset(gsum[:, :], 0.0).then_inc(mix_dve, 1)
                elif part == 1:
                    dve.tensor_tensor(kvb[:, :], out_[0:C, 0:C], k("kvblock")[0:C, :], ALU.mult).then_inc(mix_dve, 1)
                elif part == 2:
                    dve.scalar_tensor_tensor(out=m2[:, :], in0=out_[0:C, 0:C + 1], scalar=1.0 / NPOS, in1=i65[:, :],
                                             op0=ALU.mult, op1=ALU.add).then_inc(mix_dve, 1)
                else:
                    now(dve, "lproj_psum", i * GROUPS - 1)
                    dve.tensor_tensor(m65[:, :], out_[0:C + 1, 0:C], blp[:, :], ALU.add).then_inc(mix_dve, 1)

            def gp_(c, j):
                before(dve, "lproj_psum", c)
                now(dve, "uT_kept", c)
                dve.tensor_copy(utc[0:C, :], ut_img[:, bass.ds(j * GTOK, GTOK)]).then_inc(S["utc_ready"], 1)

            def gp2(c, j):
                now(dve, "gelu_ready", c)
                now(dve, "tu_ready", c)
                before(dve, "yinit_ready", c)
                dve.tensor_tensor(t2[:, :, :].rearrange("p t c -> p (t c)"), gp[:, :, :].rearrange("p t c -> p (t c)"),
                                  tu_img[:, bass.ds(j * (GT * C), GT * C)], ALU.add).then_inc(S["t2_ready"], 1)

            def statsx(c, j):
                now(dve, "t2_ready", c)
                statistics(c, "x", lambda t: t2[:, t, :])

            def gpn(c, j):
                now(dve, "x_scale", c, 0)
                before(dve, "xnT_psum", c)
                for t in range(GT):
                    last = dve.tensor_scalar(xn[:, t, :, :], t2[:, t, :].unsqueeze(1).to_broadcast([TOK, 2, C]),
                                             mv["x"][:, t, 0:1], v3[:, 4, t:t + 1], ALU.subtract, ALU.mult)
                last.then_inc(S["xn_ready"], 1)

            k_rank = k("rank")[0:TOK].unsqueeze(1).to_broadcast([TOK, GT, NE])

            def logit(c, j):
                now(dve, "logit_psum", c)
                now(dve, "x_scale", c, 1)
                dve.tensor_tensor(lg[:, 0], pB[0:TOK, 0:GT * NE].rearrange("p (t e) -> p t e", e=NE),
                                  v3[:, 5, :].unsqueeze(2).to_broadcast([TOK, GT, NE]), ALU.mult).then_inc(S["route"], 1)

            def route(c, k):
                def wide(v):
                    return v.unsqueeze(2).to_broadcast([TOK, GT, NE])

                L, M = (lambda a: lg[:, a]), (lambda a: lm[:, a])
                half, part = divmod(k - 2, 6)
                src, a = (L(1), 2) if half == 0 else (L(5), 6)
                now(dve, "route", c, k - 1)
                if k == 1:
                    last = dve.tensor_tensor(L(1), L(0), brb[:, :].unsqueeze(1).to_broadcast([TOK, GT, NE]), ALU.add)
                elif k == ROUTE_DIFF:
                    dve.tensor_tensor(M(4), M(2), M(0), ALU.subtract).then_inc(S["top_diff"], 1)
                    return
                elif part == 0:
                    last = dve.tensor_reduce(M(2 * half), src, AX, ALU.max)
                elif part == 1:
                    last = dve.tensor_tensor(L(a), src, wide(M(2 * half)), ALU.is_equal)
                elif part == 2:
                    last = dve.tensor_tensor(L(a + 1), L(a), k_rank, ALU.mult)
                elif part == 3:
                    last = dve.tensor_reduce(M(2 * half + 1), L(a + 1), AX, ALU.max)
                elif part == 4:
                    last = dve.tensor_tensor(L(a + 2), L(a + 1), wide(M(2 * half + 1)), ALU.is_equal)
                else:
                    last = dve.scalar_tensor_tensor(out=L(5), in0=L(4), scalar=-1e30, in1=L(1), op0=ALU.mult, op1=ALU.add)
                last.then_inc(S["route"], 1)

            def gates(c, j):
                L, M = (lambda a: lg[:, a]), (lambda a: lm[:, a])
                now(dve, "tanh_ready", c)
                dve.tensor_scalar(M(6), M(5), -0.5, 0.5, ALU.mult, ALU.add).then_inc(S["route"], 1)
                dve.tensor_scalar(M(7), M(5), 0.5, 0.5, ALU.mult, ALU.add).then_inc(S["route"], 1)

            def weights(c, j):
                L, M = (lambda a: lg[:, a]), (lambda a: lm[:, a])
                first = COUNTS["route"] - 4
                now(dve, "route", c, first + 1)
                dve.tensor_tensor(L(9), L(4), M(6).unsqueeze(2).to_broadcast([TOK, GT, NE]), ALU.mult).then_inc(S["route"], 1)
                dve.tensor_tensor(L(10), L(8), M(7).unsqueeze(2).to_broadcast([TOK, GT, NE]), ALU.mult).then_inc(S["route"], 1)

            def add_weights(c, j):
                L = lambda a: lg[:, a]
                now(dve, "route", c, COUNTS["route"] - 1)
                before(dve, "gateT_psum", c)
                now(dve, "yg_ready", c - 2, NE - 1)
                dve.tensor_tensor(gate[:, :, :], L(9), L(10), ALU.add).then_inc(S["gate_ready"], 1)
                dve.tensor_tensor(gate2[:, bass.ts(c % 2, 1)].rearrange("p a t e -> p (a t) e"), L(9), L(10), ALU.add)\
                    .then_inc(S["gate2_ready"], 1)

            def gbias(c, j):
                now(dve, "gbias_psum", c)
                now(dve, "y_sum", c - 2, NE - 1)
                dve.tensor_tensor(yacc[:, bass.ts(c % 2, 1), :].rearrange("p a (t c) -> p (a t) c", c=C),
                                  pB[0:TOK, 0:GT * C].rearrange("p (t c) -> p t c", c=C),
                                  t2[:, :, :], ALU.add).then_inc(S["yinit_ready"], 1)

            def split(d, j):
                now(dve, "xnT_ready", d)
                before(dve, "e1_psum", d)
                dve.tensor_copy(xs[:, :], xnt[:, :]).then_inc(S["xhi_ready"], 1)

            def split_low(d, j):
                now(dve, "xhi_ready", d)
                dve.tensor_tensor(xs[C:2 * C, :], xnt[C:2 * C, :], xs[C:2 * C, :], ALU.subtract).then_inc(S["xs_ready"], 1)

            def expert(d, e):
                if e == 0:
                    now(dve, "gate2_ready", d)
                now(dve, "e2_psum", d, e)
                now(dve, "y_sum", d - (e < 2), (e - 2) % NE)
                dve.tensor_tensor(yg[:, e % 2, :].rearrange("p (t c) -> p t c", c=C),
                                  pY[0:TOK, 0:GT * C].rearrange("p (t c) -> p t c", c=C),
                                  gate2[:, bass.ts(d % 2, 1), :, e:e + 1].rearrange("p a t e -> p (a t) e")
                                  .to_broadcast([TOK, GT, C]), ALU.mult).then_inc(S["yg_ready"], 1)

            def halves(f):
                return [lambda a, j, t=t: f(a, t) for t in range(2)]

            steps = dict(st1=ln1, z=ln1n, qbd=q_blocks, ke0=lambda a, j: expand_keys(a, 0), ke2=lambda a, j: expand_keys(a, 2),
                         ve=expand_values, x1=proj, st2=stats2, z2=z2n, hn=ln3n, t=fc2, stu=statsu, u=ut,
                         kvss=kv, kve=kvsum, kvr=deviation_recip, kvn=scale_kv, Gsum=add_G, utc=gp_, t2=gp2, stx=statsx,
                         xn=gpn, rt0=logit, tw=gates, w=weights, gate=add_weights, yinit=gbias, hi=split, lo=split_low)
            for name, f in dict(st3=stats3, rc=heads_out, rm=own_window, ow=scale_heads, on=join_windows).items():
                steps[f"{name}0"], steps[f"{name}1"] = halves(f)
            for L in "123ux":
                steps[f"mv{L}"] = lambda n, j, L=L: mean_variance(n, L)
            for part in range(1, ROUTE_DIFF + 1):
                steps[f"rt{part}"] = lambda c, j, part=part: route(c, part)
            for t in range(GT):
                steps[f"sb{t}"] = lambda a, j, t=t: add_bias(a, j, t)
                steps[f"mx{t}"] = lambda a, j, t=t: largest(a, t)
            for e in range(NE):
                steps[f"g{e}"] = lambda d, j, e=e: expert(d, e)
            for part in range(4):
                steps[f"mix{part}"] = lambda i, j, part=part: mix(i, part)
            images(dve, PLAN["dve"], steps)

        @block.gpsimd
        def _(pool):
            pool.wait_ge(setup_dve, 10)
            credit(pool, "vareps_1 vareps_2 vareps_3 vareps_u vareps_x rstd_1 rstd_2 rstd_3 rstd_u rstd_x kexp_pool "
                         "score_sub x1b_ready tu_ready x_v3 x_rstd3 x_scale y_sum")

            def rstd(n, L):
                now(pool, f"meanvar_{L}", n)
                pool.tensor_tensor(ve[L][:, :], mv[L][:, :, 1], k("eps")[0:TOK], ALU.add).then_inc(S[f"vareps_{L}"], 1)

            def power(n, L):
                now(pool, f"vareps_{L}", n)
                pool.tensor_tensor(rs[L][:, :], ve[L][:, :], k("minushalf")[0:TOK], ALU.pow).then_inc(S[f"rstd_{L}"], 1)

            def ln1(a, j):
                before(pool, "z_ready", a)
                rstd(a, "1")

            def expand_keys(a, t):
                now(pool, "kT_ready", a)
                before(pool, "score_psum", a)
                spread_keys(pool, t).then_inc(S["kexp_pool"], 1)

            def subtract(a, t):
                now(pool, "score_max", a, t)
                s = sc[:, t, :].rearrange("p (h k) -> p h k", k=WA)
                pool.tensor_tensor(s, s, mx[:, t, :].unsqueeze(2).to_broadcast([TOK, HEADS, WA]), ALU.subtract)\
                    .then_inc(S["score_sub"], 1)

            def proj(a, j):
                before(pool, "z2_ready", a)
                rstd(a, "2")

            def add_bias(a, j):
                now(pool, "x1_ready", a)
                before(pool, "t_ready", a)
                pool.tensor_tensor(x1b[:, :, :], x1[:, :, :], fc2bias[:, :].unsqueeze(1).to_broadcast([TOK, GT, C]), ALU.add)\
                    .then_inc(S["x1b_ready"], 1)

            def fc1(n, j):
                before(pool, "hn_ready", n)
                rstd(n, "3")

            def fc2(n, j):
                before(pool, "u_ready", n)
                rstd(n, "u")

            def ut(n, j):
                now(pool, "u_ready", n)
                now(pool, "t2_ready", n - GROUPS)
                pool.sem_inc(held["pool"], 1)
                pool.tensor_tensor(tu_img[:, bass.ds(j * (GT * C), GT * C)],
                                   tt[:, :, :].rearrange("p t c -> p (t c)"), u[:, :, :].rearrange("p t c -> p (t c)"),
                                   ALU.add).then_inc(S["tu_ready"], 1)

            def gp2(c, j):
                before(pool, "xn_ready", c)
                before(pool, "route", c)
                rstd(c, "x")

            def normed(c, k_):
                r = rs["x"][:, :]
                if k_ == 0:
                    now(pool, "rstd_x", c)
                    pool.tensor_tensor(v3[:, 0, :], mv["x"][:, :, 1], r, ALU.mult).then_inc(S["x_v3"], 1)
                elif k_ == 1:
                    now(pool, "x_v3", c, 0)
                    pool.tensor_tensor(v3[:, 1, :], v3[:, 0, :], r, ALU.mult).then_inc(S["x_v3"], 1)
                elif k_ == 2:
                    now(pool, "x_v3", c, 1)
                    pool.tensor_tensor(v3[:, 2, :], v3[:, 1, :], k("eps")[0:TOK], ALU.add).then_inc(S["x_v3"], 1)
                elif k_ == 3:
                    now(pool, "x_v3", c, 2)
                    pool.tensor_tensor(v3[:, 3, :], v3[:, 2, :], k("minushalf")[0:TOK], ALU.pow).then_inc(S["x_rstd3"], 1)
                else:
                    now(pool, "x_rstd3", c)
                    pool.tensor_tensor(v3[:, 4, :], v3[:, 3, :], r, ALU.mult).then_inc(S["x_scale"], 1)
                    pool.tensor_tensor(v3[:, 5, :], v3[:, 3, :], v3[:, 2, :], ALU.mult).then_inc(S["x_scale"], 1)

            def expert(d, e):
                if e == 0:
                    now(pool, "yinit_ready", d)
                else:
                    now(pool, "y_sum", d, e - 1)
                now(pool, "yg_ready", d, e)
                acc = yacc[:, bass.ts(d % 2, 1), :]
                dst = acc
                if e == NE - 1:
                    pool.wait_ge(x_out, 16 * (d + 1))
                    dst = yo[:, bass.ts(d % YBUF, 1), :]
                pool.sem_inc(held["pool"], 1)
                pool.tensor_tensor(dst, acc, yg[:, e % 2:e % 2 + 1, :], ALU.add).then_inc(S["y_sum"], 1)

            steps = dict(r1=ln1, ke1=lambda a, j: expand_keys(a, 1), ke3=lambda a, j: expand_keys(a, 3), r2=proj, x1b=add_bias,
                         r3=fc1, ru=fc2, tu=ut, rx=gp2)
            for L in "123ux":
                steps[f"pw{L}"] = lambda n, j, L=L: power(n, L)
            for part in range(5):
                steps[f"v{part}"] = lambda c, j, part=part: normed(c, part)
            for t in range(GT):
                steps[f"sub{t}"] = lambda a, j, t=t: subtract(a, t)
            for e in range(NE):
                steps[f"y{e}"] = lambda d, j, e=e: expert(d, e)
            images(pool, PLAN["pool"], steps)

        @block.scalar
        def _(act):
            act.wait_ge(setup_dve, 10)
            credit(act, "zT_ready kT_ready prob_ready pT_ready oT_ready z2T_ready hid_ready hnT_ready uT_ready uT_kept "
                        "kv_square kv_sd gelu_ready xnT_ready tanh_ready gateT_ready h_ready")

            def copy(dst, src, signal):
                act.activation(dst, src, ACT.Copy).then_inc(S[signal], 1)

            def ln1n(a, j):
                now(act, "zT_psum", a)
                before(act, "v_psum", a)
                copy(zt[0:C], pA[0:C, 0:GTOK].rearrange("p (a k) -> p a k", k=WA).unsqueeze(2)
                     .to_broadcast([C, 2 * GT, 2, WA]), "zT_ready")

            def qkv(a, j):
                now(act, "k_psum", a)
                before(act, "kexp_dve", a)
                before(act, "kexp_pool", a)
                copy(kt[:, :, :].rearrange("p t k -> p (t k)"), pO[:, 0:GT * WA], "kT_ready")

            def softmax_exp(a, j):
                now(act, "score_sub", a, GT - 1)
                before(act, "pT_psum", a)
                act.activation(pr[:, :, :].rearrange("p t c -> p (t c)"), sc[:, :, :].rearrange("p t c -> p (t c)"), ACT.Exp)\
                    .then_inc(S["prob_ready"], 1)

            def keep_pt(a, t):
                if t % 2 == 0:
                    now(act, "o_psum", a - (t == 0), 1 - t // 2)
                now(act, "pT_psum", a, t)
                copy(pt[:, t % 2].rearrange("p a c -> p (a c)"), pP[0:TOK, 0:GTOK], "pT_ready")

            def oT(a, j):
                now(act, "oT_psum", a)
                before(act, "proj_psum", a)
                copy(ot[0:C, :], pA[0:C, 0:GTOK], "oT_ready")

            def z2t(n, j):
                now(act, "z2T_psum", n)
                before(act, "fc1_psum", n)
                copy(z2t_[0:C, :], pA[0:C, 0:GTOK], "z2T_ready")

            def gelu(n, half):
                if half == 0:
                    before(act, "hnT_psum", n)
                now(act, "fc1_psum", n, half)
                act.activation(hid[:, 2 * half:2 * half + 2, :].rearrange("p t c -> p (t c)"), (pB, pA)[half][0:TOK, :],
                               ACT.Gelu).then_inc(S["hid_ready"], 1)

            def keep_hidden_T(n, half):
                if half == 0:
                    before(act, "fc2_psum", n)
                now(act, "hnT_psum", n, half)
                copy(hnt[:, 2 * half:2 * half + 2].rearrange("p t h c -> p (t h c)"), (pB, pA)[half][:, 0:GTOK], "hnT_ready")

            def ut(n, j):
                now(act, "uT_psum", n)
                before(act, "kv_psum", n)
                copy(uts[0:C, :], pA[0:C, 0:GTOK], "uT_ready")

            def keep_ut(n, j):
                now(act, "uT_psum", n)
                now(act, "utc_ready", n - GROUPS)
                copy(ut_img[:, bass.ds(j * GTOK, GTOK)], pA[0:C, 0:GTOK], "uT_kept")

            def kv(n, j):
                now(act, "kv_psum", n)
                before(act, "kv_ss", n)
                act.activation(kvsq[:, :, :].rearrange("p g d -> p (g d)"), pB[0:TOK, :], ACT.Square).then_inc(S["kv_square"], 1)

            def deviation(n, j):
                now(act, "kv_ss", n)
                before(act, "kv_se", n)
                act.activation(kvsd[:, :], kvss[:, :], ACT.Sqrt, scale=1.0 / (LD - 1)).then_inc(S["kv_sd"], 1)

            def gp_(c, j):
                now(act, "lproj_psum", c)
                before(act, "t2_ready", c)
                act.activation(gp[:, :, :].rearrange("p t c -> p (t c)"), pB[0:TOK, 0:GT * C], ACT.Gelu).then_inc(S["gelu_ready"], 1)

            def gpn(c, j):
                now(act, "xnT_psum", c)
                before(act, "logit_psum", c)
                before(act, "xs_ready", c)
                copy(xnt[:, :], pB[:, 0:GTOK], "xnT_ready")

            def route(c, j):
                now(act, "top_diff", c)
                act.activation(lm[:, 5, :], lm[:, 4, :], ACT.Tanh, scale=0.5).then_inc(S["tanh_ready"], 1)

            def gates(c, j):
                now(act, "gateT_psum", c)
                before(act, "gbias_psum", c)
                copy(gtt[:, :], pB[0:NE, 0:GTOK], "gateT_ready")

            def expert(d, b):
                if b % 2 == 0:
                    now(act, "e2_psum", d - (b < 4), (b // 2 - 2) % NE)
                now(act, "e1_psum", d, b)
                act.activation(ht[:, b % 4, :], pH[b % 2][:, 0:GTOK], ACT.Gelu, bias=be1[:, b:b + 1],
                               scale=1.0 / WSCALE).then_inc(S["h_ready"], 1)

            steps = dict(zt=ln1n, kt=qkv, ot=oT, z2t=z2t, uts=ut, utk=keep_ut, sq=kv, sd=deviation, lpg=gp_, xnt=gpn,
                         tanh=route, gtt=gates, exp=softmax_exp,
                         ge0=lambda n, j: gelu(n, 0), ge1=lambda n, j: gelu(n, 1), hnt0=lambda n, j: keep_hidden_T(n, 0),
                         hnt1=lambda n, j: keep_hidden_T(n, 1))
            for t in range(GT):
                steps[f"pt{t}"] = lambda a, j, t=t: keep_pt(a, t)
            for b in range(2 * NE):
                steps[f"h{b}"] = lambda d, j, b=b: expert(d, b)
            images(act, PLAN["act"], steps)


def layout(inputs):
    x = np.asarray(inputs["x"])
    B, H, W, _ = x.shape
    NW = H // WS
    v = {k: np.asarray(a) for k, a in inputs.items()}
    win = np.roll(x, (-SHIFT, -SHIFT), axis=(1, 2)).reshape(B, NW, WS, NW, WS, C).transpose(0, 1, 3, 2, 4, 5)
    win = win.reshape(B, NW * NW // 2, TOK, C).transpose(0, 2, 1, 3)
    lw = v["L1_attn_W_qkv"].reshape(LH, 3, LD, C).transpose(1, 0, 2, 3).reshape(3, C, C)
    lb = v["L1_attn_b_qkv"].reshape(LH, 3, LD).transpose(1, 0, 2).reshape(3, C)
    col = lambda a: a.reshape(-1, 1)
    line = lambda a: a.reshape(1, -1)
    halves = lambda a: a.reshape(2, 128, -1).transpose(1, 0, 2)
    p0, p1, p2 = "L0_conv_", "L1_attn_", "L1_ffn_"
    return dict(
        x=win, cst=constants()[0],
        wqkv=v[p0 + "qkv_w"].T, bqkv=line(v[p0 + "qkv_b"]),
        table=v[p0 + "rpb_table"], projw=v[p0 + "proj_w"].T, projb=line(v[p0 + "proj_b"]),
        fc1w=v[p0 + "fc1_w"].T, fc1b=line(v[p0 + "fc1_b"]), fc2w=halves(v[p0 + "fc2_w"].T), fc2b=line(v[p0 + "fc2_b"]),
        amask=v[p0 + "attn_mask"], rel=v[p0 + "rel_index"].reshape(-1),
        lnvecs=np.concatenate([col(v[p0 + a]) for a in ("ln1_w", "ln1_b", "ln2_w", "ln2_b")]
                              + [v[p2 + "ln_g"].T, v[p2 + "ln_b"].T], 1),
        ln3=np.concatenate([v[p0 + a].reshape(2, 128).T for a in ("ln3_w", "ln3_b")], 1),
        lwkv=np.concatenate([lw[1].T, lw[2].T], 1), lbkv=line(np.concatenate([lb[1], lb[2]])),
        lwq=np.concatenate([lw[0], col(lb[0])], 1),
        lnkvw=np.concatenate([col(v[p1 + "kln_w"]), col(v[p1 + "vln_w"])], 1),
        klnb=line(v[p1 + "kln_b"]), vlnb=line(v[p1 + "vln_b"]),
        lwp=v[p1 + "W_proj"].T, lbp=line(v[p1 + "b_proj"]),
        wr=v[p2 + "Wr"], br=v[p2 + "br"],
        w1=v[p2 + "W1"].transpose(1, 0, 2).reshape(C, NE * HID), b1=v[p2 + "b1"].reshape(2 * NE, 128).T,
        w2=v[p2 + "W2"].reshape(NE, 2, 128, C).transpose(2, 0, 1, 3).reshape(128, NE * 2, C), b2=v[p2 + "b2"],
    )


def kernel(**inputs):
    import concourse.bacc as bacc
    from concourse.bass_utils import run_bass_kernel_spmd

    B, H, W, _ = inputs["x"].shape
    nc = bacc.Bacc("TRN2", target_bir_lowering=False, num_devices=1)
    arrays, args = {}, []
    for name, a in layout(inputs).items():
        a = np.ascontiguousarray(a)
        arrays[f"in_{name}"] = a
        args.append(nc.dram_tensor(f"in_{name}", a.shape, mybir.dt.from_np(a.dtype), kind="ExternalInput").ap())
    shape = arrays["in_x"].shape
    args.append(nc.dram_tensor("out_y", shape, F32, kind="ExternalOutput").ap())
    build(nc, *args)
    r = run_bass_kernel_spmd(nc, [arrays], core_ids=[0])
    y = r.results[0]["out_y"]
    NW = H // WS
    y = y.transpose(0, 2, 1, 3).reshape(B, NW, NW, WS, WS, C).transpose(0, 1, 3, 2, 4, 5).reshape(B, H, W, C)
    return np.roll(y, (SHIFT, SHIFT), axis=(1, 2))
```
